# Optimizing a Trainium2 kernel written in Bass

```python
import numpy as np
import jax
import jax.numpy as jnp

def _softmax(x, axis=-1):
    return jax.nn.softmax(x, axis=axis)

def _gelu(x):
    return jax.nn.gelu(x, approximate=True)

def _silu(x):
    return jax.nn.silu(x)

def _sigmoid(x):
    return jax.nn.sigmoid(x)

def _layernorm(x, axis=-1, eps=1e-05):
    m = jnp.mean(x, axis=axis, keepdims=True)
    v = jnp.var(x, axis=axis, keepdims=True)
    return (x - m) / jnp.sqrt(v + eps)

def _scatter_add(tgt, idx, src, axis=0):
    return tgt.at[idx].add(src)

def _segment_sum(src, seg, n):
    return jax.ops.segment_sum(src, seg, n)
kernel_name = 'mk_decoder_preln_d1_seqx_r4_d495e4'

def setup_inputs(seed: int=0):
    np.random.seed(seed)
    _w = jnp.asarray

    def _rec_inputs():
        import jax
        import jax.numpy as jnp
        _rk = jax.random.key(seed)
        x = -0.0002928 + 1 * jax.random.normal(jax.random.fold_in(_rk, 1), (2, 1024, 256), jnp.float32)
        _lenS = 1024 - jax.random.randint(jax.random.fold_in(_rk, 7), (2,), 0, max(1, 1024 // 4) + 1, jnp.int32)
        _lenS2 = 154 - jax.random.randint(jax.random.fold_in(_rk, 8), (2,), 0, max(1, 154 // 4) + 1, jnp.int32)
        _ctx_1024P = jax.random.normal(jax.random.fold_in(_rk, 11), (2, 16, 256), jnp.float32)
        _ctx_1024c = jax.random.dirichlet(jax.random.fold_in(_rk, 511), 0.3 * jnp.ones((16,), jnp.float32), (2, 154))
        _ctx_1024t = jnp.einsum('bsk,bkd->bsd', _ctx_1024c, _ctx_1024P)
        _ctx_1024t = _ctx_1024t * jax.lax.rsqrt(jnp.mean(jnp.square(_ctx_1024t)) + 1e-12) * 0.953939
        ctx_1024 = -1.39393e-06 + 0.999914 * (_ctx_1024t + 0.3 * jax.random.normal(jax.random.fold_in(_rk, 611), (2, 154, 256), jnp.float32))
        fside_Bx16xSxS2_0 = jax.random.uniform(jax.random.fold_in(_rk, 12), (2, 16, 1024, 154), jnp.float32, 0.0, 1)
        _validS = jnp.arange(1024)[None, :] < _lenS[:, None]
        _validS2 = jnp.arange(154)[None, :] < _lenS2[:, None]
        _causal = jnp.tril(jnp.ones((1024, 1024), dtype=bool))
        mask_Bx16xSxS2_bk1 = jnp.broadcast_to(_validS2[:, None, None, :], (2, 16, 1024, 154))
        return (x, ctx_1024, fside_Bx16xSxS2_0, mask_Bx16xSxS2_bk1)
    x, ctx_1024, fside_Bx16xSxS2_0, mask_Bx16xSxS2_bk1 = _rec_inputs()

    def _L0_attn_setup():
        import jax, jax.numpy as jnp
        import numpy as np
        from functools import partial
        CHUNK = 32

        def _phi(x):
            return jax.nn.elu(x) + 1.0

        def _decay_scan(x, log_d, init):
            B, H, T, D = x.shape
            C = min(CHUNK, T)
            assert T % C == 0
            Nc = T // C
            c_idx = jnp.arange(C, dtype=x.dtype)
            lp = log_d[None, :, None, None] * c_idx[None, None, :, None]
            p = jnp.exp(lp)
            inv_p = jnp.exp(-lp)
            init_p = jnp.exp(log_d[None, :, None, None] * (c_idx + 1.0)[None, None, :, None])
            xc = x.reshape(B, H, Nc, C, D).transpose(2, 0, 1, 3, 4)

            def step(state, chunk):
                cs = jnp.cumsum(chunk * inv_p, axis=2)
                out = cs * p + state[:, :, None, :] * init_p
                return (out[:, :, -1, :], out)
            last, outs = jax.lax.scan(step, init, xc)
            out = outs.transpose(1, 2, 0, 3, 4).reshape(B, H, T, D)
            return (out, last)

        def _reference_tuple_inner(x, w_qkv, w_out, alpha, beta):
            B, T, HID = x.shape
            H = alpha.shape[0]
            D = HID // H
            qkv = x @ w_qkv
            q, k, v = jnp.split(qkv, 3, axis=-1)
            to_bhtd = lambda t: t.reshape(B, T, H, D).transpose(0, 2, 1, 3)
            q = _phi(to_bhtd(q))
            k = _phi(to_bhtd(k))
            v = to_bhtd(v)
            kv = k * v
            log_a = jnp.log(jnp.clip(jax.nn.sigmoid(alpha), 1e-08, None))
            log_b = jnp.log(jnp.clip(jax.nn.sigmoid(beta), 1e-08, None))
            z = jnp.zeros((B, H, D), dtype=x.dtype)
            run_kv_f, kv_f1 = _decay_scan(kv, log_a, z)
            run_ks_f, ks_f1 = _decay_scan(k, log_a, z)
            run_kv_s, kv_s1 = _decay_scan(kv, log_b, z)
            run_ks_s, ks_s1 = _decay_scan(k, log_b, z)
            eps = 1e-06
            den_f = jnp.clip(jnp.sum(q * run_ks_f, axis=-1, keepdims=True), eps, None)
            den_s = jnp.clip(jnp.sum(q * run_ks_s, axis=-1, keepdims=True), eps, None)
            out_f = (q * run_kv_f / den_f).transpose(0, 2, 1, 3).reshape(B, T, HID)
            out_s = (q * run_kv_s / den_s).transpose(0, 2, 1, 3).reshape(B, T, HID)
            out = jnp.concatenate([out_f, out_s], axis=-1) @ w_out
            return (out, (kv_f1, ks_f1, kv_s1, ks_s1))
        key = jax.random.key(seed)
        k1, k2, k3, k4, k5 = jax.random.split(key, 5)
        B, T, HID, H = (4, 1024, 256, 16)
        logit = lambda p: float(np.log(p / (1.0 - p)))
        return {'x': jax.random.normal(k1, (B, T, HID), dtype=jnp.float32), 'w_qkv': jax.random.normal(k2, (HID, 3 * HID), dtype=jnp.float32) * 0.02, 'w_out': jax.random.normal(k3, (2 * HID, HID), dtype=jnp.float32) * 0.02, 'alpha': jnp.full((H,), logit(0.7), dtype=jnp.float32) + 0.01 * jax.random.normal(k4, (H,), dtype=jnp.float32), 'beta': jnp.full((H,), logit(0.97), dtype=jnp.float32) + 0.01 * jax.random.normal(k5, (H,), dtype=jnp.float32)}
    _L0_attn_all = _L0_attn_setup()
    _L0_attn_in = {k: v for k, v in _L0_attn_all.items() if k in ('w_qkv', 'w_out', 'alpha', 'beta')}
    del _L0_attn_all

    def _L0_xattn_setup():
        import jax, jax.numpy as jnp
        import numpy as np
        D_MODEL, D_K, D_V, H = (256, 64, 64, 16)
        B, NQ, NK = (2, 512, 512)
        key = jax.random.key(seed)
        ks = jax.random.split(key, 14)
        xavier = lambda k, fan_in, fan_out: jax.random.uniform(k, (fan_in, fan_out), jnp.float32, -jnp.sqrt(6.0 / (fan_in + fan_out)), jnp.sqrt(6.0 / (fan_in + fan_out)))
        return {'queries': jax.random.normal(ks[0], (B, NQ, D_MODEL), jnp.float32), 'keys': jax.random.normal(ks[1], (B, NK, D_MODEL), jnp.float32), 'values': jax.random.normal(ks[2], (B, NK, D_MODEL), jnp.float32), 'attention_weights': jax.random.uniform(ks[3], (B, H, NQ, NK), jnp.float32), 'attention_mask': jax.random.randint(ks[4], (B, H, NQ, NK), 0, 2).astype(jnp.bool_), 'Wq': xavier(ks[5], D_MODEL, H * D_K), 'bq': jnp.zeros((H * D_K,), jnp.float32), 'Wk': xavier(ks[6], D_MODEL, H * D_K), 'bk': jnp.zeros((H * D_K,), jnp.float32), 'Wv': xavier(ks[7], D_MODEL, H * D_V), 'bv': jnp.zeros((H * D_V,), jnp.float32), 'Wo': xavier(ks[8], H * D_V, D_MODEL), 'bo': jnp.zeros((D_MODEL,), jnp.float32)}
    _L0_xattn_all = _L0_xattn_setup()
    _L0_xattn_in = {k: v for k, v in _L0_xattn_all.items() if k in ('Wq', 'bq', 'Wk', 'bk', 'Wv', 'bv', 'Wo', 'bo')}
    del _L0_xattn_all

    def _L0_ffn_setup():
        import jax, jax.numpy as jnp
        import numpy as np
        from jax import lax
        D = 256
        H = 352
        E = 8
        K = 2
        ROUTER_SCALE = 1.0

        def _expert(x, w1, b1, w3, b3, w2, b2):
            h = jax.nn.silu((x @ w1 + b1) * (x @ w3 + b3))
            return h @ w2 + b2
        key = jax.random.key(seed)
        ks = jax.random.split(key, 16)
        s = 0.02
        inp = {'x': jax.random.normal(ks[0], (2, 512, D), dtype=jnp.float32), 'gate_w': jax.random.normal(ks[1], (E, D), dtype=jnp.float32) * s, 'gate_b': jax.random.normal(ks[2], (E,), dtype=jnp.float32) * s, 'w1': jax.random.normal(ks[3], (E, D, H), dtype=jnp.float32) * s, 'b1': jax.random.normal(ks[4], (E, H), dtype=jnp.float32) * s, 'w3': jax.random.normal(ks[5], (E, D, H), dtype=jnp.float32) * s, 'b3': jax.random.normal(ks[6], (E, H), dtype=jnp.float32) * s, 'w2': jax.random.normal(ks[7], (E, H, D), dtype=jnp.float32) * s, 'b2': jax.random.normal(ks[8], (E, D), dtype=jnp.float32) * s, 'sw1': jax.random.normal(ks[9], (D, H), dtype=jnp.float32) * s, 'sb1': jax.random.normal(ks[10], (H,), dtype=jnp.float32) * s, 'sw3': jax.random.normal(ks[11], (D, H), dtype=jnp.float32) * s, 'sb3': jax.random.normal(ks[12], (H,), dtype=jnp.float32) * s, 'sw2': jax.random.normal(ks[13], (H, D), dtype=jnp.float32) * s, 'sb2': jax.random.normal(ks[14], (D,), dtype=jnp.float32) * s}
        return inp
    _L0_ffn_all = _L0_ffn_setup()
    _L0_ffn_in = {k: v for k, v in _L0_ffn_all.items() if k in ('gate_w', 'gate_b', 'w1', 'b1', 'w3', 'b3', 'w2', 'b2', 'sw1', 'sb1', 'sw3', 'sb3', 'sw2', 'sb2')}
    del _L0_ffn_all
    return {'x': x, 'ctx_1024': ctx_1024, 'fside_Bx16xSxS2_0': fside_Bx16xSxS2_0, 'mask_Bx16xSxS2_bk1': mask_Bx16xSxS2_bk1, 'L0_attn_w_qkv': _L0_attn_in['w_qkv'], 'L0_attn_w_out': _L0_attn_in['w_out'], 'L0_attn_alpha': _L0_attn_in['alpha'], 'L0_attn_beta': _L0_attn_in['beta'], 'L0_xattn_Wq': _L0_xattn_in['Wq'], 'L0_xattn_bq': _L0_xattn_in['bq'], 'L0_xattn_Wk': _L0_xattn_in['Wk'], 'L0_xattn_bk': _L0_xattn_in['bk'], 'L0_xattn_Wv': _L0_xattn_in['Wv'], 'L0_xattn_bv': _L0_xattn_in['bv'], 'L0_xattn_Wo': _L0_xattn_in['Wo'], 'L0_xattn_bo': _L0_xattn_in['bo'], 'L0_ffn_gate_w': _L0_ffn_in['gate_w'], 'L0_ffn_gate_b': _L0_ffn_in['gate_b'], 'L0_ffn_w1': _L0_ffn_in['w1'], 'L0_ffn_b1': _L0_ffn_in['b1'], 'L0_ffn_w3': _L0_ffn_in['w3'], 'L0_ffn_b3': _L0_ffn_in['b3'], 'L0_ffn_w2': _L0_ffn_in['w2'], 'L0_ffn_b2': _L0_ffn_in['b2'], 'L0_ffn_sw1': _L0_ffn_in['sw1'], 'L0_ffn_sb1': _L0_ffn_in['sb1'], 'L0_ffn_sw3': _L0_ffn_in['sw3'], 'L0_ffn_sb3': _L0_ffn_in['sb3'], 'L0_ffn_sw2': _L0_ffn_in['sw2'], 'L0_ffn_sb2': _L0_ffn_in['sb2']}

def reference(x, ctx_1024, fside_Bx16xSxS2_0, mask_Bx16xSxS2_bk1, L0_attn_w_qkv, L0_attn_w_out, L0_attn_alpha, L0_attn_beta, L0_xattn_Wq, L0_xattn_bq, L0_xattn_Wk, L0_xattn_bk, L0_xattn_Wv, L0_xattn_bv, L0_xattn_Wo, L0_xattn_bo, L0_ffn_gate_w, L0_ffn_gate_b, L0_ffn_w1, L0_ffn_b1, L0_ffn_w3, L0_ffn_b3, L0_ffn_w2, L0_ffn_b2, L0_ffn_sw1, L0_ffn_sb1, L0_ffn_sw3, L0_ffn_sb3, L0_ffn_sw2, L0_ffn_sb2):
    import jax
    import jax.numpy as jnp

    def _L0_attn_ref(x, w_qkv, w_out, alpha, beta):
        import jax, jax.numpy as jnp
        import numpy as np
        from functools import partial
        CHUNK = 32

        def _phi(x):
            return jax.nn.elu(x) + 1.0

        def _decay_scan(x, log_d, init):
            B, H, T, D = x.shape
            C = min(CHUNK, T)
            assert T % C == 0
            Nc = T // C
            c_idx = jnp.arange(C, dtype=x.dtype)
            lp = log_d[None, :, None, None] * c_idx[None, None, :, None]
            p = jnp.exp(lp)
            inv_p = jnp.exp(-lp)
            init_p = jnp.exp(log_d[None, :, None, None] * (c_idx + 1.0)[None, None, :, None])
            xc = x.reshape(B, H, Nc, C, D).transpose(2, 0, 1, 3, 4)

            def step(state, chunk):
                cs = jnp.cumsum(chunk * inv_p, axis=2)
                out = cs * p + state[:, :, None, :] * init_p
                return (out[:, :, -1, :], out)
            last, outs = jax.lax.scan(step, init, xc)
            out = outs.transpose(1, 2, 0, 3, 4).reshape(B, H, T, D)
            return (out, last)

        def _reference_tuple_inner(x, w_qkv, w_out, alpha, beta):
            B, T, HID = x.shape
            H = alpha.shape[0]
            D = HID // H
            qkv = x @ w_qkv
            q, k, v = jnp.split(qkv, 3, axis=-1)
            to_bhtd = lambda t: t.reshape(B, T, H, D).transpose(0, 2, 1, 3)
            q = _phi(to_bhtd(q))
            k = _phi(to_bhtd(k))
            v = to_bhtd(v)
            kv = k * v
            log_a = jnp.log(jnp.clip(jax.nn.sigmoid(alpha), 1e-08, None))
            log_b = jnp.log(jnp.clip(jax.nn.sigmoid(beta), 1e-08, None))
            z = jnp.zeros((B, H, D), dtype=x.dtype)
            run_kv_f, kv_f1 = _decay_scan(kv, log_a, z)
            run_ks_f, ks_f1 = _decay_scan(k, log_a, z)
            run_kv_s, kv_s1 = _decay_scan(kv, log_b, z)
            run_ks_s, ks_s1 = _decay_scan(k, log_b, z)
            eps = 1e-06
            den_f = jnp.clip(jnp.sum(q * run_ks_f, axis=-1, keepdims=True), eps, None)
            den_s = jnp.clip(jnp.sum(q * run_ks_s, axis=-1, keepdims=True), eps, None)
            out_f = (q * run_kv_f / den_f).transpose(0, 2, 1, 3).reshape(B, T, HID)
            out_s = (q * run_kv_s / den_s).transpose(0, 2, 1, 3).reshape(B, T, HID)
            out = jnp.concatenate([out_f, out_s], axis=-1) @ w_out
            return (out, (kv_f1, ks_f1, kv_s1, ks_s1))
        return _reference_tuple_inner(x, w_qkv, w_out, alpha, beta)[0]

    def _L0_xattn_ref(queries, keys, values, attention_weights, attention_mask, Wq, bq, Wk, bk, Wv, bv, Wo, bo):
        import jax, jax.numpy as jnp
        import numpy as np
        D_MODEL, D_K, D_V, H = (256, 64, 64, 16)
        B, NQ, NK = (2, 512, 512)
        b_s, nq, _ = queries.shape
        nk = keys.shape[1]
        q = (queries @ Wq + bq).reshape(b_s, nq, H, D_K).transpose(0, 2, 1, 3)
        k = (keys @ Wk + bk).reshape(b_s, nk, H, D_K).transpose(0, 2, 1, 3)
        v = (values @ Wv + bv).reshape(b_s, nk, H, D_V).transpose(0, 2, 1, 3)
        att = jnp.einsum('bhqd,bhkd->bhqk', q, k) / jnp.sqrt(jnp.float32(D_K))
        att = att * attention_weights
        att = jnp.where(attention_mask, -jnp.inf, att)
        att = jax.nn.softmax(att, axis=-1)
        out = jnp.einsum('bhqk,bhkd->bhqd', att, v)
        out = out.transpose(0, 2, 1, 3).reshape(b_s, nq, H * D_V)
        return out @ Wo + bo

    def _L0_ffn_ref(x, gate_w, gate_b, w1, b1, w3, b3, w2, b2, sw1, sb1, sw3, sb3, sw2, sb2):
        import jax, jax.numpy as jnp
        import numpy as np
        from jax import lax
        D = 256
        H = 352
        E = 8
        K = 2
        ROUTER_SCALE = 1.0

        def _expert(x, w1, b1, w3, b3, w2, b2):
            h = jax.nn.silu((x @ w1 + b1) * (x @ w3 + b3))
            return h @ w2 + b2
        shape = x.shape
        xf = x.reshape(-1, D)
        T = xf.shape[0]
        scores = jax.nn.softmax(xf @ gate_w.T, axis=-1)
        biased = scores + gate_b
        _, idx = lax.top_k(biased, K)
        w = jnp.take_along_axis(scores, idx, axis=-1) * ROUTER_SCALE
        rw = jnp.zeros((T, E), dtype=xf.dtype).at[jnp.arange(T)[:, None], idx].add(w)
        h = jax.nn.silu((jnp.einsum('td,edh->teh', xf, w1) + b1) * (jnp.einsum('td,edh->teh', xf, w3) + b3))
        oe = jnp.einsum('teh,ehd->ted', h, w2) + b2
        y = jnp.einsum('te,ted->td', rw, oe)
        z = _expert(xf, sw1, sb1, sw3, sb3, sw2, sb2)
        return (y + z).reshape(shape)
    x = x + _L0_attn_ref(_layernorm(x, axis=-1), L0_attn_w_qkv, L0_attn_w_out, L0_attn_alpha, L0_attn_beta)
    x = x + _L0_xattn_ref(_layernorm(x, axis=-1), ctx_1024, ctx_1024, fside_Bx16xSxS2_0, mask_Bx16xSxS2_bk1, L0_xattn_Wq, L0_xattn_bq, L0_xattn_Wk, L0_xattn_bk, L0_xattn_Wv, L0_xattn_bv, L0_xattn_Wo, L0_xattn_bo)
    x = x + _L0_ffn_ref(_layernorm(x, axis=-1), L0_ffn_gate_w, L0_ffn_gate_b, L0_ffn_w1, L0_ffn_b1, L0_ffn_w3, L0_ffn_b3, L0_ffn_w2, L0_ffn_b2, L0_ffn_sw1, L0_ffn_sb1, L0_ffn_sw3, L0_ffn_sb3, L0_ffn_sw2, L0_ffn_sb2)
    return x

_drawn_inputs = setup_inputs


def setup_inputs(seed=0):
    import zlib

    import numpy as np

    out = dict(_drawn_inputs(seed))
    spreads = {'L0_xattn_bq': (0.0, 0.8),
     'L0_xattn_bk': (0.0, 0.8),
     'L0_xattn_bv': (0.0, 0.1),
     'L0_xattn_bo': (0.0, 0.1)}
    factors = {'fside_Bx16xSxS2_0': 3.592,
     'L0_attn_w_qkv': 8.0,
     'L0_attn_w_out': 8.0,
     'L0_attn_alpha': 37.011,
     'L0_attn_beta': 8.0,
     'L0_ffn_gate_w': 8.0,
     'L0_ffn_gate_b': 8.0,
     'L0_ffn_w1': 8.0,
     'L0_ffn_b1': 8.0,
     'L0_ffn_w3': 8.0,
     'L0_ffn_b3': 8.0,
     'L0_ffn_w2': 8.0,
     'L0_ffn_b2': 40.556,
     'L0_ffn_sw1': 3.199,
     'L0_ffn_sb1': 35.541,
     'L0_ffn_sw3': 3.2,
     'L0_ffn_sb3': 37.946,
     'L0_ffn_sw2': 3.21,
     'L0_ffn_sb2': 25.92}
    for name, (base, spread) in spreads.items():
        noise = np.random.default_rng([zlib.crc32(name.encode()), seed]).standard_normal(out[name].shape)
        drawn = base * np.exp(spread * noise) if base else spread * noise
        out[name] = jnp.asarray(drawn.astype(out[name].dtype))
    for name, factor in factors.items():
        out[name] = (out[name] * factor).astype(out[name].dtype)
    return out
```

```python
from contextlib import ExitStack

import numpy as np
import concourse.bass as bass
from concourse import mybir

ALU = mybir.AluOpType
ACT = mybir.ActivationFunctionType
AX = mybir.AxisListType
F32 = mybir.dt.float32
U8 = mybir.dt.uint8

P = 128
B = 2
S = 1024
D = 256
N = B * S
NT = N // P
NCH = 4
CT = 512
H = 16
SK = 154
HK = 160
PW = 2 * SK
NE = 8
F = 352
MT = [(0, 128), (128, 128), (256, 96)]
BIG = 3.0e38


class Engine:

    def __init__(self, sem):
        self.sem, self.count, self.items = sem, 0, []

    def do(self, fn, *waits, sig=True):
        self.items.append((waits, fn, sig))
        self.count += sig
        return (self.sem, self.count)

    def dma(self, sem, total, out, in_, *waits):
        self.items.append((waits, lambda e: e.dma_start(out, in_).then_inc(sem, 16), False))
        return (sem, total)

    def wait(self, *waits):
        self.items.append((waits, None, False))

    def play(self, eng):
        seen = {}
        for waits, fn, sig in self.items:
            for sem, value in waits:
                if seen.get(id(sem), 0) < value:
                    eng.wait_ge(sem, value)
                    seen[id(sem)] = value
            if fn is not None:
                ins = fn(eng)
                if sig:
                    ins.then_inc(self.sem, 1)


def decoder(nc, A, out):
    with ExitStack() as ctx:
        def sb(name, shape, dt=F32):
            return ctx.enter_context(nc.sbuf_tensor(name, shape, dt))

        sems = [0]

        def sem():
            sems[0] += 1
            return ctx.enter_context(nc.semaphore(f"s{sems[0]}"))

        pe, dve, act, pool, sp = (Engine(sem()) for _ in range(5))
        banks = [ctx.enter_context(nc.psum_tensor(f"bank{i}", [P, 512], F32)) for i in range(8)]
        freed = [()] * 8
        turn = [0]

        def bank():
            i = turn[0] % 8
            turn[0] += 1
            return i, banks[i], freed[i]

        x = sb("x", [P, NT, D])
        ident = sb("ident", [P, P])
        sel = sb("sel", [P, 4, 32])
        selT = sb("selT", [32, 4, P])
        cst = sb("cst", [P, 2])
        xnT = sb("xnT", [P, 2, 2, CT])
        xn = sb("xn", [P, 4, D])
        st = sb("st", [P, 4, 6])
        mv = sb("mv", [P, 4, 2])
        sd = sb("sd", [P, 4])
        rs = sb("rs", [P, 4])
        dec = sb("dec", [P, 2, 2])
        dec2 = sb("dec2", [P, 2, 2])
        wq = sb("wq", [P, 2, 1024])
        wo = sb("wo", [P, 8, D])
        bqk = sb("bqk", [P, 2, 8])
        bq8 = sb("bq8", [P, 8])
        boB = sb("boB", [P, D])
        kbd = sb("kbd", [P, B, 8, PW])
        vbd = sb("vbd", [P, B, 3, 8, P])
        gw = sb("gw", [P, 2, NE])
        gbB = sb("gbB", [P, NE])
        iot = sb("iot", [P, NE])
        R3 = sb("R3", [P, 7040])
        wqkv = R3[:, 0:1536].rearrange("p (k n) -> p k n", k=2)
        wout = R3[:, 1536:2560].rearrange("p (k n) -> p k n", k=4)
        wk = R3[:, 2560:4608].rearrange("p (k n) -> p k n", k=2)
        wv = R3[:, 4608:6656].rearrange("p (k n) -> p k n", k=2)
        fs = R3[:, 0:2 * 2464].rearrange("p (s h k) -> p s h k", s=2, h=H)
        mk = R3[:, 4928:4928 + 2 * 616].bitcast(U8).rearrange("p (s h k) -> p s h k", s=2, h=H)
        R2 = sb("R2", [P, 5120])
        ctxT = R2[:, 0:616].rearrange("p (k n) -> p k n", k=2)
        ctxV = R2[:, 616:616 + 1536].rearrange("p (k b t n) -> p k b t n", k=2, b=B, t=3)
        bvB = R2[:, 2152:3176]
        pT = R2[:, 0:3072].rearrange("p (s j t q) -> p s j t q", s=2, j=2, t=3)
        oT = R2[:, 3072:5120].rearrange("p (j q) -> p j q", j=8)
        R1 = sb("R1", [P, 15872])
        qb = R1[:, 0:2048].rearrange("p (k n) -> p k n", k=2)
        kb = R1[:, 2048:4096].rearrange("p (k n) -> p k n", k=2)
        kvb = R1[:, 4096:6144].rearrange("p (k n) -> p k n", k=2)
        run = R1[:, 6144:14336].rearrange("p (w j n) -> p w j n", w=2, j=4)
        tmp = R1[:, 14336:15360]
        den = R1[0:32, 15360:15872]
        qT = R1[:, 0:4096].rearrange("p (j n) -> p j n", j=8)
        att = R1[:, 4096:4096 + 4 * 2560].rearrange("p (s h k) -> p s h k", s=4, h=H)
        mx = sb("mx", [P, 4, 4, H])
        x3T = R1[:, 0:4096].rearrange("p (k n) -> p k n", k=2)
        hA = R1[:, 4096:4096 + 3072].rearrange("p (s m n) -> p s m n", s=2, m=3)
        hZ = R1[:, 7168:7168 + 3072].rearrange("p (s m n) -> p s m n", s=2, m=3)
        ffw = R1[:, 10240:10240 + 2 * 2176].rearrange("p (s n) -> p s n", s=2)
        b13 = sb("b13", [P, 2, 9, 3])
        b2s = sb("b2s", [9, D])
        lg = sb("lg", [P, NT, NE])
        ga = sb("ga", [P, NT, NE])
        gbb = sb("gbb", [P, NT, NE])
        gc = sb("gc", [P, NT, NE])
        gm = sb("gm", [P, NT])
        rw = sb("rw", [P, NT, 9])
        rwT = R2[0:9, 0:2048].rearrange("p (t n) -> p t n", t=NT)

        def load(q, parts, *waits):
            s = sem()
            total = 16 * len(parts)
            for o, i in parts:
                q.dma(s, total, o, i, *waits)
            return (s, total)

        xv = A["x"].rearrange("b (t p) d -> p (b t) d", p=P)
        outv = out.rearrange("b (t p) d -> p (b t) d", p=P)
        t_x = [load(sp, [(x[:, 4 * c:4 * c + 4, :], xv[:, 4 * c:4 * c + 4, :])]) for c in range(NCH)]
        t_cst = load(act, [(ident[:, :], A["ident"]), (sel[:, :, :], A["sel"]), (selT[:, :, :], A["selT"]),
                           (dec[:, :, :], A["decay"]), (cst[:, :], A["cst"]), (iot[:, :], A["iota"])])
        t_wqkv = load(sp, [(wqkv, A["L0_attn_w_qkv"].rearrange("(k p) n -> p k n", p=P))])
        t_wout = load(sp, [(wout, A["L0_attn_w_out"].rearrange("(k p) n -> p k n", p=P))])
        t_ctx = load(act, [(ctxT, A["ctxT"].rearrange("(k p) n -> p k n", p=P)),
                           (R2[:, 616:2152].rearrange("p (k n) -> p k n", k=2),
                            A["ctxV"].rearrange("(k p) n -> p k n", p=P)),
                           (bqk[:, :, :], A["bqk"]),
                           (bvB, A["L0_xattn_bv"].rearrange("(a n) -> a n", a=1).broadcast_to([P, 1024]))])
        t_wk = load(sp, [(wk, A["L0_xattn_Wk"].rearrange("(k p) n -> p k n", p=P))])
        t_wv = load(sp, [(wv, A["L0_xattn_Wv"].rearrange("(k p) n -> p k n", p=P))])
        t_wq = load(sp, [(wq[:, :, :], A["L0_xattn_Wq"].rearrange("(k p) n -> p k n", p=P))])
        t_wo = load(sp, [(wo[:, :, :], A["L0_xattn_Wo"].rearrange("(k p) n -> p k n", p=P)),
                         (boB[:, :], A["L0_xattn_bo"].rearrange("(a n) -> a n", a=1).broadcast_to([P, D]))])
        t_sm = load(act, [(gw[:, :, :], A["gateT"]),
                          (gbB[:, :], A["L0_ffn_gate_b"].rearrange("(a n) -> a n", a=1).broadcast_to([P, NE])),
                          (b13[:, :, :, :], A["b13"]),
                          (b2s[0:8, :], A["L0_ffn_b2"]),
                          (b2s[8:9, :], A["L0_ffn_sb2"].rearrange("(a n) -> a n", a=1))])

        t_kz = pool.do(lambda e: e.memset(kbd[:, :, :, :], 0.0))
        t_vz = pool.do(lambda e: e.memset(vbd[:, :, :, :, :], 0.0))
        t_rw1 = pool.do(lambda e: e.memset(rw[:, :, 8:9], 1.0))

        xn_free = [()]
        xnT_free = [(), ()]

        def norm(c, dst, ready, dst_free):
            for i in range(4):
                t = 4 * c + i
                a = dve.do(lambda e, t=t, i=i: e.bn_stats(st[:, i, :], x[:, t, :]), *ready)
                a = dve.do(lambda e, i=i: e.bn_aggr(mv[:, i, :], st[:, i, :]), a)
            s = act.do(lambda e: e.activation(sd[:, :], mv[:, :, 1], ACT.Sqrt, bias=cst[:, 0:1]), a, t_cst)
            r = dve.do(lambda e: e.reciprocal(rs[:, :], sd[:, :]), s)
            for i in range(4):
                t = 4 * c + i
                a = dve.do(lambda e, t=t, i=i: e.tensor_scalar(xn[:, i, :], x[:, t, :], mv[:, i, 0:1], rs[:, i:i + 1],
                                                                ALU.subtract, ALU.mult), r, *xn_free[0])
            done = []
            for k in range(2):
                n, ps, fr = bank()
                for i in range(4):
                    w = pe.do(lambda e, ps=ps, i=i, k=k: e.transpose(ps[:, i * P:(i + 1) * P],
                                                                     xn[:, i, k * P:(k + 1) * P], ident[:, :]),
                              a, t_cst, *fr, sig=(i == 3))
                g = act.do(lambda e, ps=ps, k=k: e.copy(dst[:, k, :], ps[:, :]), w, *dst_free)
                freed[n] = (g,)
                done.append(g)
            xn_free[0] = (w,)
            return done

        t_d = act.do(lambda e: e.activation(dec2[:, :, :], dec[:, :, :], ACT.Exp, scale=-1.0), t_cst)
        t_d = dve.do(lambda e: e.tensor_scalar(dec2[:, :, :], dec2[:, :, :], 1.0, None, ALU.add), t_d)
        t_d = dve.do(lambda e: e.reciprocal(dec2[:, :, :], dec2[:, :, :]), t_d)
        t_d = dve.do(lambda e: e.tensor_scalar(dec2[:, :, :], dec2[:, :, :], 1e-8, None, ALU.max), t_d)

        tmp_free = [()]
        den_free = [()]
        scratch_free = [()]

        def attention(b):
            xT = []
            for h in range(2):
                c = 2 * b + h
                xT.append(norm(c, xnT[:, h, :, :], (t_x[c],), xnT_free[h]))
            used = []
            last_mm = [None, None]

            def project(blk, h):
                n, ps, fr = bank()
                for k in range(2):
                    w = pe.do(lambda e, ps=ps, k=k, blk=blk, h=h: e.matmul(
                        ps[:, :], wqkv[:, k, blk * P:(blk + 1) * P], xnT[:, h, k, :],
                        start=(k == 0), stop=(k == 1)), *xT[h], t_wqkv, *fr, sig=(k == 1))
                last_mm[h] = w
                return n, ps, w

            tk = {}
            for name, first, buf in (("k", 2, kb), ("q", 0, qb)):
                for blk in range(2):
                    for h in range(2):
                        n, ps, w = project(first + blk, h)
                        cols = slice(h * CT, (h + 1) * CT)
                        e1 = act.do(lambda e, ps=ps: e.activation(tmp[:, 0:512], ps[:, :], ACT.Exp), w, *tmp_free[0],
                                    *scratch_free[0])
                        e2 = act.do(lambda e, ps=ps: e.activation(tmp[:, 512:1024], ps[:, :], ACT.Relu))
                        freed[n] = (e2,)
                        g = dve.do(lambda e, buf=buf, blk=blk, cols=cols: e.scalar_tensor_tensor(
                            out=buf[:, blk, cols], in0=tmp[:, 0:512], scalar=1.0, in1=tmp[:, 512:1024],
                            op0=ALU.min, op1=ALU.add), e2)
                        tmp_free[0] = (g,)
                        tk[name, blk] = g
                        if name == "k":
                            n, ps, w = project(4 + blk, h)
                            g = dve.do(lambda e, ps=ps, blk=blk, cols=cols: e.tensor_tensor(
                                kvb[:, blk, cols], ps[:, :], kb[:, blk, cols], ALU.mult), w, g)
                            freed[n] = (g,)
                            tk["kv", blk] = g
            for h in range(2):
                xnT_free[h] = (last_mm[h],)
            qk, qkv = {}, {}
            for blk in range(2):
                for f in range(2):
                    j = 2 * f + blk
                    for w, src, into in ((0, kb, qk), (1, kvb, qkv)):
                        r = dve.do(lambda e, w=w, j=j, f=f, blk=blk, src=src: e.tensor_tensor_scan(
                            run[:, w, j, :], dec2[:, f, blk:blk + 1].broadcast_to([P, S]), src[:, blk, :], 0.0,
                            ALU.mult, ALU.add), t_d, tk["k", blk], tk["kv", blk])
                        eng = dve if w == 0 else pool
                        into[j] = eng.do(lambda e, w=w, j=j, blk=blk: e.tensor_tensor(
                            run[:, w, j, :], run[:, w, j, :], qb[:, blk, :], ALU.mult), r, tk["q", blk])
            for h in range(2):
                c = 2 * b + h
                cols = slice(h * CT, (h + 1) * CT)
                n, ps, fr = bank()
                for i, j in enumerate((0, 2, 1, 3)):
                    w = pe.do(lambda e, ps=ps, i=i, j=j, cols=cols: e.matmul(
                        ps[0:32, :], sel[:, j, :], run[:, 0, j, cols], start=(i == 0), stop=(i == 3)),
                        qk[j], t_cst, *fr, sig=(i == 3))
                d = dve.do(lambda e, ps=ps: e.tensor_scalar(den, ps[0:32, :], 1e-6, None, ALU.max), w, *den_free[0])
                freed[n] = (d,)
                d = dve.do(lambda e: e.reciprocal(den, den), d)
                on = []
                for j in range(4):
                    n, ps, fr = bank()
                    w = pe.do(lambda e, ps=ps, j=j: e.matmul(ps[:, :], selT[:, j, :], den, start=True, stop=True),
                              d, t_cst, *fr)
                    g = dve.do(lambda e, ps=ps, j=j, cols=cols: e.tensor_tensor(
                        run[:, 1, j, cols], ps[:, :], run[:, 1, j, cols], ALU.mult), w, qkv[j])
                    freed[n] = (g,)
                    on.append(g)
                den_free[0] = (w,)
                for t in range(4):
                    n, ps, fr = bank()
                    for j in range(4):
                        w = pe.do(lambda e, ps=ps, j=j, t=t, h=h: e.matmul(
                            ps[:, 0:D], run[:, 1, j, h * CT + t * P:h * CT + (t + 1) * P], wout[:, j, :],
                            start=(j == 0), stop=(j == 3)), on[j], t_wout, *fr, sig=(j == 3))
                    g = dve.do(lambda e, ps=ps, c=c, t=t: e.tensor_tensor(
                        x[:, 4 * c + t, :], ps[:, 0:D], x[:, 4 * c + t, :], ALU.add), w)
                    freed[n] = (g,)
                t_x[c] = g
            scratch_free[0] = (w, g)

        attention(0)

        t_bq8 = dve.do(lambda e: e.tensor_scalar(bq8[:, :], bqk[:, 0, :], 0.125, None, ALU.mult), t_ctx)
        for j in range(8):
            n, ps, fr = bank()
            for k in range(2):
                w = pe.do(lambda e, ps=ps, k=k, j=j: e.matmul(ps[:, 0:PW], wk[:, k, j * P:(j + 1) * P], ctxT[:, k, :],
                                                              start=(k == 0), stop=(k == 1)),
                          t_ctx, t_wk, *fr, sig=(k == 1))
            for b in range(B):
                for r in range(2):
                    rows = slice(64 * r, 64 * r + 64)
                    t_k = act.do(lambda e, ps=ps, j=j, b=b, r=r, rows=rows: e.activation(
                        kbd[rows, b, j, r * SK:(r + 1) * SK], ps[rows, b * SK:(b + 1) * SK], ACT.Identity,
                        bias=bqk[rows, 1, j:j + 1]), w, t_kz)
            freed[n] = (t_k,)
        for b in range(B):
            for t, segs in enumerate([[(0, 128, 0)], [(0, 32, 0), (32, 64, 1), (64, 128, 1)], [(0, 58, 1)]]):
                for half in range(2):
                    n, ps, fr = bank()
                    for k in range(2):
                        w = pe.do(lambda e, ps=ps, k=k, b=b, t=t, half=half: e.matmul(
                            ps[:, :], ctxV[:, k, b, t, :], wv[:, k, half * 512:(half + 1) * 512],
                            start=(k == 0), stop=(k == 1)), t_ctx, t_wv, *fr, sig=(k == 1))
                    for lo, hi, r in segs:
                        t_v = dve.do(lambda e, ps=ps, b=b, t=t, half=half, lo=lo, hi=hi, r=r: e.tensor_tensor(
                            vbd[lo:hi, b, t, 4 * half:4 * half + 4, 64 * r:64 * r + 64],
                            ps[lo:hi, :].rearrange("p (j r d) -> p j r d", j=4, r=2)[:, :, r, :],
                            bvB[lo:hi, half * 512:(half + 1) * 512].rearrange("p (j r d) -> p j r d", j=4, r=2)[
                                :, :, r, :], ALU.add), w, t_vz)
                    freed[n] = (t_v,)

        attention(1)

        t_az = pool.do(lambda e: e.memset(att[:, :, :, SK:HK], 0.0), *scratch_free[0])
        fs_sem = [sem() for _ in range(2)]
        fs_free = [(scratch_free[0] + (t_k, t_v))] * 2
        att_free = [scratch_free[0] + (t_az,)] * 4
        q_free = [scratch_free[0]]
        normed = {}

        def queries(c):
            xT = norm(c, xnT[:, c % 2, :, :], (t_x[c],), xnT_free[c % 2])
            add = [pool.do(lambda e, t=t: e.tensor_tensor(x[:, t, :], x[:, t, :], boB[:, :], ALU.add), *xT, t_wo)
                   for t in range(4 * c, 4 * c + 4)]
            normed[c] = (add[-1],)
            for j in range(8):
                n, ps, fr = bank()
                for k in range(2):
                    w = pe.do(lambda e, ps=ps, k=k, j=j, c=c: e.matmul(
                        ps[:, :], wq[:, k, j * P:(j + 1) * P], xnT[:, c % 2, k, :], start=(k == 0), stop=(k == 1)),
                        *xT, t_wq, *fr, sig=(k == 1))
                g = act.do(lambda e, ps=ps, j=j: e.activation(qT[:, j, :], ps[:, :], ACT.Identity,
                                                              bias=bq8[:, j:j + 1], scale=0.125),
                           w, t_bq8, *q_free[0])
                freed[n] = (g,)
            xnT_free[c % 2] = (w,)
            return (g,)

        probs = {}

        def scores(t, tq):
            b, s, a4 = t // 8, t % 2, t % 4
            tf = (fs_sem[s], 32 * (t // 2 + 1))
            sp.dma(fs_sem[s], 0, fs[:, s, :, :], A["fside"][t], *fs_free[s])
            sp.dma(fs_sem[s], 0, mk[:, s, :, :], A["mask"][t])
            for j in range(8):
                n, ps, fr = bank()
                w = pe.do(lambda e, ps=ps, j=j, b=b, t=t: e.matmul(
                    ps[:, 0:PW], qT[:, j, (t % 4) * P:(t % 4 + 1) * P], kbd[:, b, j, :], start=True, stop=True),
                    *tq, t_k, *fr)
                g = dve.do(lambda e, ps=ps, j=j, s=s, a4=a4: e.tensor_tensor(
                    att[:, a4, 2 * j:2 * j + 2, 0:SK], ps[:, 0:PW].rearrange("p (r k) -> p r k", r=2),
                    fs[:, s, 2 * j:2 * j + 2, :], ALU.mult), w, tf, *att_free[a4])
                freed[n] = (g,)
            if t % 4 == 3:
                q_free[0] = (w,)
            g = dve.do(lambda e: e.scalar_tensor_tensor(
                out=att[:, a4, :, 0:SK], in0=mk[:, s, :, :], scalar=-BIG, in1=att[:, a4, :, 0:SK],
                op0=ALU.mult, op1=ALU.add), g)
            fs_free[s] = (g,)
            g = dve.do(lambda e: e.tensor_reduce(mx[:, a4, 0, :], att[:, a4, :, 0:SK], AX.X, ALU.max), g)
            g = dve.do(lambda e: e.tensor_scalar(mx[:, a4, 1, :], mx[:, a4, 0, :], -1.0e38, -BIG,
                                                 ALU.is_le, ALU.mult), g)
            g = dve.do(lambda e: e.scalar_tensor_tensor(
                out=mx[:, a4, 1, :], in0=mx[:, a4, 1, :], scalar=BIG, in1=mx[:, a4, 0, :],
                op0=ALU.mult, op1=ALU.subtract), g)
            for h in range(H):
                e1 = act.do(lambda e, h=h: e.activation(att[:, a4, h, 0:SK], att[:, a4, h, 0:SK], ACT.Exp,
                                                        bias=mx[:, a4, 1, h:h + 1], accum_out=mx[:, a4, 2, h:h + 1]), g)
            g = dve.do(lambda e: e.reciprocal(mx[:, a4, 3, :], mx[:, a4, 2, :]), e1)
            probs[t] = pool.do(lambda e: e.tensor_tensor(
                att[:, a4, :, 0:SK], att[:, a4, :, 0:SK],
                mx[:, a4, 3, :].rearrange("p (h a) -> p h a", a=1).broadcast_to([P, H, SK]), ALU.mult), g, e1)

        pT_free = [(t_k, t_v)] * 2
        oT_free = [(t_k, t_v)]

        def values(u):
            b = u // 4
            oc = []
            for jj in range(4):
                s = jj % 2
                ev = []
                n2, ps2, fr2 = bank()
                for i in range(2):
                    j = 2 * jj + i
                    n, ps, fr = bank()
                    for tt, (lo, m) in enumerate([(0, 128), (128, 128), (256, 58)]):
                        for q in range(2):
                            a4 = (2 * u + q) % 4
                            o = ps[0:m, (2 * tt + q) * P:(2 * tt + q + 1) * P] if tt < 2 else \
                                ps2[0:m, (2 * i + q) * P:(2 * i + q + 1) * P]
                            w = pe.do(lambda e, o=o, a4=a4, j=j, lo=lo, m=m: e.transpose(
                                o, att[:, a4, 2 * j:2 * j + 2, :].rearrange("p r k -> p (r k)")[:, lo:lo + m],
                                ident[:, :]), probs[2 * u + q], *fr, *fr2, sig=(q == 1))
                        if tt == 1:
                            g = act.do(lambda e, ps=ps, s=s, i=i: e.copy(
                                pT[:, s, i, 0:2, :], ps[:, :].rearrange("p (t q) -> p t q", t=2)), w, *pT_free[s])
                            freed[n] = (g,)
                            ev.append(g)
                g = dve.do(lambda e, ps2=ps2, s=s: e.tensor_copy(
                    pT[0:58, s, :, 2, :], ps2[0:58, :].rearrange("p (i q) -> p i q", i=2)), w, *pT_free[s])
                freed[n2] = (g,)
                ev.append(g)
                n, ps, fr = bank()
                for i in range(2):
                    for tt, m in enumerate([128, 128, 58]):
                        w2 = pe.do(lambda e, ps=ps, i=i, tt=tt, m=m, jj=jj, s=s: e.matmul(
                            ps[:, i * 256:(i + 1) * 256], vbd[0:m, b, tt, 2 * jj + i, :], pT[0:m, s, i, tt, :],
                            start=(tt == 0), stop=(tt == 2)), *ev, t_v, *fr, sig=(tt == 2))
                pT_free[s] = (w2,)
                g = dve.do(lambda e, ps=ps, jj=jj: e.tensor_copy(
                    oT[:, 2 * jj:2 * jj + 2, :], ps[:, :].rearrange("p (i q) -> p i q", i=2)), w2, *oT_free[0])
                freed[n] = (g,)
                oc.append(g)
            for q in range(2):
                att_free[(2 * u + q) % 4] = (w,)
            for q in range(2):
                t = 2 * u + q
                n, ps, fr = bank()
                for j in range(8):
                    w = pe.do(lambda e, ps=ps, j=j, q=q: e.matmul(
                        ps[:, 0:D], oT[:, j, q * P:(q + 1) * P], wo[:, j, :], start=(j == 0), stop=(j == 7)),
                        oc[j // 2], t_wo, *fr, sig=(j == 7))
                g = dve.do(lambda e, ps=ps, t=t: e.tensor_tensor(x[:, t, :], ps[:, 0:D], x[:, t, :], ALU.add),
                           w, *normed[t // 4])
                freed[n] = (g,)
            oT_free[0] = (w,)
            t_x[u // 2] = g

        for c in range(NCH):
            tq = queries(c)
            for i in range(4):
                scores(4 * c + i, tq)
                if i % 2 == 1:
                    values(2 * c + i // 2)
        phase = (w_all := pe.do(lambda e: e.transpose(banks[turn[0] % 8][:, 0:P], ident[:, :], ident[:, :]),
                                *freed[turn[0] % 8]),)

        x3 = []
        for c in range(NCH):
            x3.append(norm(c, x3T[:, :, c * CT:(c + 1) * CT], (t_x[c],), phase + tuple(att_free[0])))
        for t in range(NT):
            n, ps, fr = bank()
            for k in range(2):
                w = pe.do(lambda e, ps=ps, k=k, t=t: e.matmul(ps[:, 0:NE], x3T[:, k, t * P:(t + 1) * P], gw[:, k, :],
                                                              start=(k == 0), stop=(k == 1)),
                          *x3[t // 4], t_sm, *fr, sig=(k == 1))
            g = dve.do(lambda e, ps=ps, t=t: e.tensor_copy(lg[:, t, :], ps[:, 0:NE]), w)
            freed[n] = (g,)

        def per_token(v):
            return v.rearrange("p (t a) -> p t a", a=1).broadcast_to([P, NT, NE])

        def per_expert(v):
            return v.rearrange("p (a n) -> p a n", a=1).broadcast_to([P, NT, NE])

        def dstep(fn, *waits):
            return dve.do(fn, (dve.sem, dve.count), *waits)

        dstep(lambda e: e.tensor_reduce(gm[:, :], lg[:, :, :], AX.X, ALU.max))
        g = dstep(lambda e: e.tensor_tensor(lg[:, :, :], lg[:, :, :], per_token(gm[:, :]), ALU.subtract))
        w = act.do(lambda e: e.activation(lg[:, :, :], lg[:, :, :], ACT.Exp), g)
        dstep(lambda e: e.tensor_reduce(gm[:, :], lg[:, :, :], AX.X, ALU.add), w)
        dstep(lambda e: e.reciprocal(gm[:, :], gm[:, :]))
        dstep(lambda e: e.tensor_tensor(lg[:, :, :], lg[:, :, :], per_token(gm[:, :]), ALU.mult))
        dstep(lambda e: e.tensor_tensor(ga[:, :, :], lg[:, :, :], per_expert(gbB[:, :]), ALU.add), t_sm)
        for i in range(2):
            dstep(lambda e: e.tensor_reduce(gm[:, :], ga[:, :, :], AX.X, ALU.max))
            dstep(lambda e: e.tensor_tensor(gbb[:, :, :], ga[:, :, :], per_token(gm[:, :]), ALU.is_ge))
            dstep(lambda e: e.tensor_tensor(gbb[:, :, :], gbb[:, :, :], per_expert(iot[:, :]), ALU.mult), t_cst)
            dstep(lambda e: e.tensor_reduce(gm[:, :], gbb[:, :, :], AX.X, ALU.max))
            o = (gc if i == 0 else gbb)
            dstep(lambda e, o=o: e.tensor_tensor(o[:, :, :], per_expert(iot[:, :]), per_token(gm[:, :]), ALU.is_equal))
            if i == 0:
                dstep(lambda e: e.scalar_tensor_tensor(out=ga[:, :, :], in0=gc[:, :, :], scalar=-BIG, in1=ga[:, :, :],
                                                       op0=ALU.mult, op1=ALU.add))
        dstep(lambda e: e.tensor_tensor(gc[:, :, :], gc[:, :, :], gbb[:, :, :], ALU.add))
        t_rw = dstep(lambda e: e.tensor_tensor(rw[:, :, 0:8], gc[:, :, :], lg[:, :, :], ALU.mult), t_rw1)
        for t in range(NT):
            n, ps, fr = bank()
            w = pe.do(lambda e, ps=ps, t=t: e.transpose(ps[0:9, 0:P], rw[:, t, :], ident[:, :]), t_rw, *fr)
            g = act.do(lambda e, ps=ps, t=t: e.copy(rwT[:, t, :], ps[0:9, 0:P]), w)
            freed[n] = (g,)
            n, ps, fr = bank()
            w = pe.do(lambda e, ps=ps, t=t: e.matmul(ps[:, 0:D], rwT[:, t, :], b2s[:, :], start=True, stop=True),
                      g, t_sm, *fr)
            g = dve.do(lambda e, ps=ps, t=t: e.tensor_tensor(x[:, t, :], ps[:, 0:D], x[:, t, :], ALU.add), w)
            freed[n] = (g,)
        y = [(g,)] * NT

        ff_sem = [sem() for _ in range(2)]
        ff_free = [phase, phase]
        hA_free = [phase, phase]
        hZ_free = [phase, phase]
        turn_h = 0
        t_out = sem()
        for ex in range(9):
            s = ex % 2
            w1 = ffw[:, s, 0:704].rearrange("p (k n) -> p k n", k=2)
            w3 = ffw[:, s, 704:1408].rearrange("p (k n) -> p k n", k=2)
            w2 = ffw[:, s, 1408:2176].rearrange("p (k n) -> p k n", k=3)
            a1, a3, a2 = ((A["L0_ffn_w1"][ex], A["L0_ffn_w3"][ex], A["L0_ffn_w2"][ex]) if ex < 8 else
                          (A["L0_ffn_sw1"], A["L0_ffn_sw3"], A["L0_ffn_sw2"]))
            tw = (ff_sem[s], 64 * (ex // 2 + 1))
            sp.dma(ff_sem[s], 0, w1, a1.rearrange("(k p) n -> p k n", p=P), *ff_free[s])
            sp.dma(ff_sem[s], 0, w3, a3.rearrange("(k p) n -> p k n", p=P))
            sp.dma(ff_sem[s], 0, w2[:, 0:2, :], a2[0:256].rearrange("(k p) n -> p k n", p=P))
            sp.dma(ff_sem[s], 0, w2[0:96, 2, :], a2[256:352])
            for c in range(NCH):
                hs = turn_h % 2
                turn_h += 1
                zs = []
                for m, (lo, mw) in enumerate(MT):
                    pair = []
                    for wm in (w1, w3):
                        n, ps, fr = bank()
                        for k in range(2):
                            w = pe.do(lambda e, ps=ps, k=k, wm=wm, lo=lo, mw=mw, c=c: e.matmul(
                                ps[0:mw, :], wm[:, k, lo:lo + mw], x3T[:, k, c * CT:(c + 1) * CT],
                                start=(k == 0), stop=(k == 1)), tw, *x3[c], *fr, sig=(k == 1))
                        pair.append((n, ps, w))
                    n, ps, w = pair[0]
                    ga_ = act.do(lambda e, ps=ps, hs=hs, m=m, mw=mw, ex=ex: e.activation(
                        hA[0:mw, hs, m, :], ps[0:mw, :], ACT.Identity, bias=b13[0:mw, 0, ex, m:m + 1]),
                        w, t_sm, *hA_free[hs])
                    freed[n] = (ga_,)
                    n, ps, w = pair[1]
                    gd = dve.do(lambda e, ps=ps, hs=hs, m=m, mw=mw, ex=ex: e.scalar_tensor_tensor(
                        out=hZ[0:mw, hs, m, :], in0=ps[0:mw, :], scalar=b13[0:mw, 1, ex, m:m + 1],
                        in1=hA[0:mw, hs, m, :], op0=ALU.add, op1=ALU.mult), w, ga_, t_sm, *hZ_free[hs])
                    freed[n] = (gd,)
                    zs.append(act.do(lambda e, hs=hs, m=m, mw=mw: e.activation(
                        hZ[0:mw, hs, m, :], hZ[0:mw, hs, m, :], ACT.Silu), gd))
                hA_free[hs] = (gd,)
                for i in range(4):
                    t = 4 * c + i
                    n, ps, fr = bank()
                    for m, (lo, mw) in enumerate(MT):
                        w = pe.do(lambda e, ps=ps, m=m, mw=mw, i=i, hs=hs, w2=w2: e.matmul(
                            ps[:, 0:D], hZ[0:mw, hs, m, i * P:(i + 1) * P], w2[0:mw, m, :],
                            start=(m == 0), stop=(m == 2)), zs[m], tw, *fr, sig=(m == 2))
                    g = dve.do(lambda e, ps=ps, t=t, ex=ex: e.scalar_tensor_tensor(
                        out=x[:, t, :], in0=ps[:, 0:D], scalar=rw[:, t, ex:ex + 1], in1=x[:, t, :],
                        op0=ALU.mult, op1=ALU.add), w, t_rw, *y[t])
                    freed[n] = (g,)
                    y[t] = (g,)
                hZ_free[hs] = (w,)
                if ex == 8:
                    sp.dma(t_out, 0, outv[:, 4 * c:4 * c + 4, :], x[:, 4 * c:4 * c + 4, :], g)
            ff_free[s] = (w,)
        sp.wait((t_out, 16 * NCH))

        block = ctx.enter_context(nc.Block())

        @block.sync
        def _(eng):
            sp.play(eng)

        @block.scalar
        def _(eng):
            act.play(eng)

        @block.gpsimd
        def _(eng):
            pool.play(eng)

        @block.vector
        def _(eng):
            dve.play(eng)

        @block.tensor
        def _(eng):
            pe.play(eng)


def layout(inputs):
    a = {k: np.ascontiguousarray(v) for k, v in inputs.items()}
    o = {k: a[k] for k in ("x", "L0_attn_w_qkv", "L0_attn_w_out", "L0_xattn_Wq", "L0_xattn_Wk", "L0_xattn_Wv",
                           "L0_xattn_Wo", "L0_xattn_bv", "L0_xattn_bo", "L0_ffn_gate_b", "L0_ffn_w1", "L0_ffn_w3",
                           "L0_ffn_w2", "L0_ffn_b2", "L0_ffn_sw1", "L0_ffn_sw3", "L0_ffn_sw2", "L0_ffn_sb2")}
    ctx = a["ctx_1024"]
    o["ctxT"] = np.ascontiguousarray(ctx.reshape(B * SK, D).T)
    cv = np.zeros((D, B, 3, P), ctx.dtype)
    for b in range(B):
        t = ctx[b].T
        cv[:, b, 0, :] = t[:, 0:128]
        cv[:, b, 1, 0:26] = t[:, 128:154]
        cv[:, b, 1, 32:128] = t[:, 0:96]
        cv[:, b, 2, 0:58] = t[:, 96:154]
    o["ctxV"] = cv.reshape(D, B * 3 * P)
    o["fside"] = np.ascontiguousarray(
        a["fside_Bx16xSxS2_0"].reshape(B, H, 8, P, SK).transpose(0, 2, 3, 1, 4)).reshape(NT, P, H, SK)
    o["mask"] = np.ascontiguousarray(
        a["mask_Bx16xSxS2_bk1"].reshape(B, H, 8, P, SK).transpose(0, 2, 3, 1, 4)).reshape(NT, P, H, SK)
    ab = np.stack([a["L0_attn_alpha"], a["L0_attn_beta"]])
    o["decay"] = np.ascontiguousarray(np.repeat(ab, 16, axis=1).reshape(2, 2, P).transpose(2, 0, 1))
    bqk = np.stack([a["L0_xattn_bq"], a["L0_xattn_bk"]])
    o["bqk"] = np.ascontiguousarray(bqk.reshape(2, 8, P).transpose(2, 0, 1))
    o["gateT"] = np.ascontiguousarray(a["L0_ffn_gate_w"].T.reshape(2, P, NE).transpose(1, 0, 2))
    b13 = np.zeros((2, 9, 384), np.float32)
    b13[0, 0:8, 0:F], b13[0, 8, 0:F] = a["L0_ffn_b1"], a["L0_ffn_sb1"]
    b13[1, 0:8, 0:F], b13[1, 8, 0:F] = a["L0_ffn_b3"], a["L0_ffn_sb3"]
    o["b13"] = np.ascontiguousarray(b13.reshape(2, 9, 3, P).transpose(3, 0, 1, 2))
    sel = np.zeros((P, 4, 32), np.float32)
    for j in range(4):
        for p in range(P):
            sel[p, j, 8 * j + p // 16] = 1.0
    o["sel"] = sel
    o["selT"] = np.ascontiguousarray(sel.transpose(2, 1, 0))
    o["ident"] = np.eye(P, dtype=np.float32)
    o["cst"] = np.full((P, 2), 1e-5, np.float32)
    o["iota"] = np.tile(np.arange(8, 0, -1).astype(np.float32), (P, 1))
    return o


def kernel(**inputs):
    import concourse.bacc as _bacc
    from concourse.bass_utils import run_bass_kernel_spmd as _run

    nc = _bacc.Bacc("TRN2", target_bir_lowering=False, num_devices=1)
    arrays, aps = {}, {}
    for name, a in layout(inputs).items():
        arrays[f"in_{name}_dram"] = a
        aps[name] = nc.dram_tensor(f"in_{name}_dram", a.shape, mybir.dt.from_np(a.dtype), kind="ExternalInput").ap()
    out = nc.dram_tensor("out_0_dram", (B, S, D), F32, kind="ExternalOutput").ap()
    decoder(nc, aps, out)
    r = _run(nc, [arrays], core_ids=[0])
    return r.results[0]["out_0_dram"]
```

```python
from contextlib import ExitStack

import numpy as np
import concourse.bass as bass
from concourse import mybir

ALU = mybir.AluOpType
ACT = mybir.ActivationFunctionType
AX = mybir.AxisListType
F32 = mybir.dt.float32
U8 = mybir.dt.uint8
I32 = mybir.dt.int32
U32 = mybir.dt.uint32

P = 128
B = 2
S = 1024
D = 256
N = B * S
NT = N // P
NCH = 4
CT = 512
H = 16
SK = 154
HK = 160
PW = 2 * SK
NE = 8
F = 352
MT = [(0, 128), (128, 128), (256, 96)]
BIG = 3.0e38
RG = 17 * P
NS = (2 * N + NE * (P - 1)) // P
XW = D + 1
XROWS = NE * RG + 7 * P
ZROWS = 2 * N + NE * P + 7 * P


class Engine:

    def __init__(self, sem):
        self.sem, self.count, self.items = sem, 0, []

    def do(self, fn, *waits, sig=True):
        self.items.append((waits, fn, sig))
        self.count += sig
        return (self.sem, self.count)

    def dma(self, sem, total, out, in_, *waits):
        self.items.append((waits, lambda e: e.dma_start(out, in_).then_inc(sem, 16), False))
        return (sem, total)

    def wait(self, *waits):
        self.items.append((waits, None, False))

    def play(self, eng):
        seen = {}
        for waits, fn, sig in self.items:
            for sem, value in waits:
                if seen.get(id(sem), 0) < value:
                    eng.wait_ge(sem, value)
                    seen[id(sem)] = value
            if fn is not None:
                ins = fn(eng)
                if sig:
                    ins.then_inc(self.sem, 1)


def decoder(nc, A, xs, zs, out):
    with ExitStack() as ctx:
        def sb(name, shape, dt=F32):
            return ctx.enter_context(nc.sbuf_tensor(name, shape, dt))

        sems = [0]

        def sem():
            sems[0] += 1
            return ctx.enter_context(nc.semaphore(f"s{sems[0]}"))

        pe, dve, act, pool, sp = (Engine(sem()) for _ in range(5))
        banks = [ctx.enter_context(nc.psum_tensor(f"bank{i}", [P, 512], F32)) for i in range(8)]
        freed = [()] * 8
        turn = [0]

        def bank():
            i = turn[0] % 8
            turn[0] += 1
            return i, banks[i], freed[i]

        x = sb("x", [P, NT, D])
        ident = sb("ident", [P, P])
        ones = sb("ones", [P, P])
        cst = sb("cst", [P, 2])
        xn = sb("xn", [P, 4, XW])
        xnT = sb("xnT", [P, 3, 2, CT])
        st = sb("st", [P, 4, 6])
        mv = sb("mv", [P, 4, 2])
        sd = sb("sd", [P, 4])
        rs = sb("rs", [P, 4])
        dec = sb("dec", [P, 2, 2])
        dec2 = sb("dec2", [P, 2, 2])
        carry = sb("carry", [P, 2, 8])
        wq = sb("wq", [P, 2, 1024])
        wo = sb("wo", [P, 8, D])
        bqk = sb("bqk", [P, 2, 8])
        bq8 = sb("bq8", [P, 8])
        boB = sb("boB", [P, D])
        mx = sb("mx", [P, 4, 4, H])
        gw = sb("gw", [P, 2, NE])
        gbB = sb("gbB", [P, NE])
        iot = sb("iot", [P, NE])
        eoff = sb("eoff", [P, NE])
        slot = sb("slot", [P, NS])
        tokid = sb("tokid", [P, NT, 2], I32)
        b13 = sb("b13", [P, 2, 3])
        sw1 = sb("sw1", [P, 2, F])
        sw3 = sb("sw3", [P, 2, F])
        sw2 = sb("sw2", [P, 3, D])
        hA = sb("hA", [P, 256])
        hZ = sb("hZ", [P, 3, 256])
        lg = sb("lg", [P, 4, NE])
        ga = sb("ga", [P, 4, NE])
        gm = sb("gm", [P, 4])
        o1 = sb("o1", [P, NT, NE])
        o2 = sb("o2", [P, NT, NE])
        gt = sb("gt", [P, 4, NE])
        cnt = sb("cnt", [P, 5, NE])
        posf = sb("posf", [P, 2, 4])
        pos = sb("pos", [P, NCH, 2, 4], I32)
        wsel = sb("wsel", [P, 2, NT])
        nti = sb("nti", [P, NE], I32)
        ntf = sb("ntf", [P, NE])
        end = sb("end", [P, NE])
        se = sb("se", [P, 3, NS])
        sei = sb("sei", [P, 2, NS], I32)
        prow = sb("prow", [P, NE], I32)
        KV = sb("KV", [P, 2 * 8 * PW + 2 * 3 * 8 * P])
        kbd = KV[:, 0:4928].rearrange("p (b j n) -> p b j n", b=B, j=8)
        vbd = KV[:, 4928:11072].rearrange("p (b t j n) -> p b t j n", b=B, t=3, j=8)
        eb = KV[:, 0:NE * 960]
        R3 = sb("R3", [P, 6656])
        wqkv = R3[:, 0:1536].rearrange("p (k n) -> p k n", k=2)
        wk = R3[:, 1536:3584].rearrange("p (k n) -> p k n", k=2)
        wv = R3[:, 3584:5632].rearrange("p (k n) -> p k n", k=2)
        wout = R3[:, 5632:6656].rearrange("p (k n) -> p k n", k=4)
        fs = R3[:, 0:2 * 2464].rearrange("p (s h k) -> p s h k", s=2, h=H)
        mk = R3[:, 4928:4928 + 2 * 616].bitcast(U8).rearrange("p (s h k) -> p s h k", s=2, h=H)
        sb2B = R3[:, 6160:6416]
        tri = R3[:, 6416:6544]
        ew2 = R3[:, 0:NE * 768]
        R2 = sb("R2", [P, 5120])
        ctxT = R2[:, 0:616].rearrange("p (k n) -> p k n", k=2)
        ctxV = R2[:, 616:2152].rearrange("p (k b t n) -> p k b t n", k=2, b=B, t=3)
        bvB = R2[:, 2152:3176]
        sel = R2[:, 3176:3688].rearrange("p (j n) -> p j n", j=4)
        selT = R2[:, 3688:4200].rearrange("p (j n) -> p j n", j=4)
        pT = R2[:, 0:3072].rearrange("p (s j t q) -> p s j t q", s=2, j=2, t=3)
        oT = R2[:, 3072:5120].rearrange("p (j q) -> p j q", j=8)
        xsl = R2[:, 0:6 * XW].rearrange("p (s n) -> p s n", s=6)
        xsT = R2[:, 1542:2054].rearrange("p (s k q) -> p s k q", s=2, k=2)
        sA = R2[:, 2054:2758].rearrange("p (s n) -> p s n", s=2)
        sZ = R2[:, 2758:3462].rearrange("p (s n) -> p s n", s=2)
        sT = R2[:, 3462:4230].rearrange("p (s m q) -> p s m q", s=2, m=3)
        cmp_ = R2[:, 4230:4230 + NS * NE].rearrange("p (s n) -> p s n", s=NS)
        R1 = sb("R1", [P, 12800])
        qb = R1[:, 0:1024].rearrange("p (k n) -> p k n", k=2)
        kb = R1[:, 1024:2048].rearrange("p (k n) -> p k n", k=2)
        kvb = R1[:, 2048:3072].rearrange("p (k n) -> p k n", k=2)
        runs = [R1[:, a:a + 4096].rearrange("p (w j n) -> p w j n", w=2, j=4) for a in (3072, 8704)]
        tmp = R1[:, 7168:8192]
        den = R1[:, 8192:8704]
        qT = R1[:, 0:2048].rearrange("p (j n) -> p j n", j=8)
        att = R1[:, 2048:12288].rearrange("p (s h k) -> p s h k", s=4, h=H)
        ew13 = R1[:, 0:NE * 1408]
        sY = R1[:, 11264:12288].rearrange("p (s n) -> p s n", s=4)
        zb = R1[:, 0:8192].rearrange("p (c w t n) -> p c w t n", c=NCH, w=2, t=4)

        def load(q, parts, *waits):
            s = sem()
            total = 16 * len(parts)
            for o, i in parts:
                q.dma(s, total, o, i, *waits)
            return (s, total)

        def rows(v, n):
            return v.rearrange("(a n) -> a n", a=1).broadcast_to([P, n])

        xv = A["x"].rearrange("b (t p) d -> p (b t) d", p=P)
        outv = out.rearrange("b (t p) d -> p (b t) d", p=P)
        t_ctx = load(act, [(ctxT, A["ctxT"].rearrange("(k p) n -> p k n", p=P)),
                           (bqk[:, :, :], A["bqk"]), (ident[:, :], A["ident"]), (cst[:, :], A["cst"])])
        t_x = [load(sp, [(x[:, i:i + 2, :], xv[:, i:i + 2, :]) for i in (0, 2)])]
        t_wk = load(sp, [(wk, A["L0_xattn_Wk"].rearrange("(k p) n -> p k n", p=P))])
        t_wqkv = load(sp, [(wqkv, A["L0_attn_w_qkv"].rearrange("(k p) n -> p k n", p=P))])
        t_cst = load(act, [(dec[:, :, :], A["decay"]), (sel, A["sel"]), (selT, A["selT"])])
        for c in range(1, NCH):
            t_x.append(load(sp, [(x[:, 4 * c:4 * c + 4, :], xv[:, 4 * c:4 * c + 4, :])]))
        t_ctxV = load(act, [(R2[:, 616:2152].rearrange("p (k n) -> p k n", k=2),
                             A["ctxV"].rearrange("(k p) n -> p k n", p=P)),
                            (bvB, rows(A["L0_xattn_bv"], 1024))])
        t_wv = load(sp, [(wv, A["L0_xattn_Wv"].rearrange("(k p) n -> p k n", p=P))])
        t_wout = load(sp, [(wout, A["L0_attn_w_out"].rearrange("(k p) n -> p k n", p=P))])
        t_wq = load(sp, [(wq[:, :, :], A["L0_xattn_Wq"].rearrange("(k p) n -> p k n", p=P))])
        t_wo = load(sp, [(wo[:, :, :], A["L0_xattn_Wo"].rearrange("(k p) n -> p k n", p=P)),
                         (boB[:, :], rows(A["L0_xattn_bo"], D))])
        t_sm = load(sp, [(gw[:, :, :], A["gateT"]), (gbB[:, :], rows(A["L0_ffn_gate_b"], NE)),
                         (b13[:, :, :], A["b13"]),
                         (iot[:, :], A["iota"]), (eoff[:, :], A["eoff"]),
                         (slot[:, :], A["slot"]), (tokid[:, :, :], A["tokid"]),
                         (sw1[:, :, :], A["L0_ffn_sw1"].rearrange("(k p) n -> p k n", p=P)),
                         (sw3[:, :, :], A["L0_ffn_sw3"].rearrange("(k p) n -> p k n", p=P)),
                         (sw2[:, 0:2, :], A["L0_ffn_sw2"][0:256].rearrange("(k p) n -> p k n", p=P)),
                         (sw2[0:96, 2, :], A["L0_ffn_sw2"][256:352])])
        xs_sem = sem()
        xs_total = [0]
        xp_sem = sem()
        sp.dma(xp_sem, 16, xs[NE * RG:XROWS, :], A["pad"][NE * P:15 * P, :])

        t_kz = pool.do(lambda e: e.memset(kbd, 0.0))
        t_vz = pool.do(lambda e: e.memset(vbd, 0.0))
        t_on = pool.do(lambda e: e.memset(ones[:, :], 1.0))
        t_c0 = pool.do(lambda e: e.memset(cnt[:, 4, :], 0.0))

        xn_free = [()]
        ring = [0]
        xnT_free = [(), (), ()]

        def norm(c, ready):
            for i in range(4):
                t = 4 * c + i
                a = dve.do(lambda e, t=t, i=i: e.bn_stats(st[:, i, :], x[:, t, :]), *ready)
                a = dve.do(lambda e, i=i: e.bn_aggr(mv[:, i, :], st[:, i, :]), a)
            s = act.do(lambda e: e.activation(sd[:, :], mv[:, :, 1], ACT.Sqrt, bias=cst[:, 0:1]), a, t_ctx)
            r = dve.do(lambda e: e.reciprocal(rs[:, :], sd[:, :]), s)
            for i in range(4):
                t = 4 * c + i
                a = dve.do(lambda e, t=t, i=i: e.tensor_scalar(xn[:, i, 0:D], x[:, t, :], mv[:, i, 0:1],
                                                                rs[:, i:i + 1], ALU.subtract, ALU.mult),
                           r, *xn_free[0])
            xn_free[0] = ()
            return a

        def turned(a):
            r = ring[0] % 3
            ring[0] += 1
            done = []
            for k in range(2):
                n, ps, fr = bank()
                for i in range(4):
                    w = pe.do(lambda e, ps=ps, i=i, k=k: e.transpose(
                        ps[:, i * P:(i + 1) * P], xn[:, i, k * P:(k + 1) * P], ident[:, :]),
                        a, t_ctx, *fr, sig=(i == 3))
                g = act.do(lambda e, ps=ps, k=k, r=r: e.copy(xnT[:, r, k, :], ps[:, :]), w, *xnT_free[r])
                freed[n] = (g,)
                done.append(g)
            xn_free[0] += (w,)
            return r, tuple(done)

        decayed = []

        def decays():
            t_d = act.do(lambda e: e.activation(dec2[:, :, :], dec[:, :, :], ACT.Exp, scale=-1.0), t_cst)
            t_d = dve.do(lambda e: e.tensor_scalar(dec2[:, :, :], dec2[:, :, :], 1.0, None, ALU.add), t_d)
            t_d = dve.do(lambda e: e.reciprocal(dec2[:, :, :], dec2[:, :, :]), t_d)
            decayed.append(dve.do(lambda e: e.tensor_scalar(dec2[:, :, :], dec2[:, :, :], 1e-8, None, ALU.max), t_d))

        tmp_free = [()]
        den_free = [()]
        run_free = [(), ()]
        chunk_free = [()]
        carried = [None]
        lin = {}

        def scan(c, rT):
            r, xT = rT
            run = runs[c % 2]

            def project(blk):
                n, ps, fr = bank()
                for k in range(2):
                    w = pe.do(lambda e, ps=ps, k=k, blk=blk: e.matmul(
                        ps[:, :], wqkv[:, k, blk * P:(blk + 1) * P], xnT[:, r, k, :],
                        start=(k == 0), stop=(k == 1)), *xT, t_wqkv, *fr, sig=(k == 1))
                return n, ps, w

            tk = {}
            for name, first, buf in (("k", 2, kb), ("q", 0, qb)):
                for blk in range(2):
                    n, ps, w = project(first + blk)
                    act.do(lambda e, ps=ps: e.activation(tmp[:, 0:512], ps[:, :], ACT.Exp), w, *tmp_free[0])
                    e2 = act.do(lambda e, ps=ps: e.activation(tmp[:, 512:1024], ps[:, :], ACT.Relu))
                    freed[n] = (e2,)
                    g = dve.do(lambda e, buf=buf, blk=blk: e.scalar_tensor_tensor(
                        out=buf[:, blk, :], in0=tmp[:, 0:512], scalar=1.0, in1=tmp[:, 512:1024],
                        op0=ALU.min, op1=ALU.add), e2, *chunk_free[0])
                    tmp_free[0] = (g,)
                    tk[name, blk] = g
                    if name == "k":
                        n, ps, w = project(4 + blk)
                        g = dve.do(lambda e, ps=ps, blk=blk: e.tensor_tensor(
                            kvb[:, blk, :], ps[:, :], kb[:, blk, :], ALU.mult), w, g, *chunk_free[0])
                        freed[n] = (g,)
                        tk["kv", blk] = g
            xnT_free[r] = (w,)
            rt = {}
            for blk in range(2):
                for f in range(2):
                    j = 2 * f + blk
                    for w, src in ((0, kb), (1, kvb)):
                        init = 0.0 if c % 2 == 0 else carry[:, w, j:j + 1]
                        more = () if c % 2 == 0 else (carried[0],)
                        rt[w, j] = dve.do(lambda e, w=w, j=j, f=f, blk=blk, src=src, init=init: e.tensor_tensor_scan(
                            run[:, w, j, :], dec2[:, f, blk:blk + 1].broadcast_to([P, CT]), src[:, blk, :], init,
                            ALU.mult, ALU.add), decayed[0], tk["k", blk], tk["kv", blk], *run_free[c % 2], *more)
            more = ()
            if c % 2 == 0:
                carried[0] = dve.do(lambda e: e.tensor_copy(carry[:, :, 0:4], run[:, :, :, CT - 1]), rt[1, 3])
                more = (carried[0],)
            qk = {}
            for w in range(2):
                for j in range(4):
                    eng = pool if w == 1 else dve
                    qk[w, j] = eng.do(lambda e, w=w, j=j: e.tensor_tensor(
                        run[:, w, j, :], run[:, w, j, :], qb[:, j % 2, :], ALU.mult),
                        rt[w, j], tk["q", j % 2], *more)
            chunk_free[0] = (qk[1, 2], qk[1, 3])
            lin[c] = qk

        dens = {}
        shared = {}

        def summed(c):
            run = runs[c % 2]
            qk = lin[c]
            n, ps, fr = bank()
            for j in range(4):
                w = pe.do(lambda e, ps=ps, j=j: e.matmul(ps[:, :], sel[:, j, :], run[:, 0, j, :],
                                                         start=(j == 0), stop=(j == 3)),
                          qk[0, j], t_cst, *fr, sig=(j == 3))
            d = dve.do(lambda e, ps=ps: e.tensor_scalar(den, ps[:, :], 1e-6, None, ALU.max), w, *den_free[0])
            freed[n] = (d,)
            dens[c] = dve.do(lambda e: e.reciprocal(den, den), d)

        def divided(c):
            run = runs[c % 2]
            qk, d = lin[c], dens[c]
            on = shared[c] = []
            for j in range(4):
                n, ps, fr = bank()
                w = pe.do(lambda e, ps=ps, j=j: e.matmul(ps[:, :], selT[:, j, :], den, start=True, stop=True),
                          d, t_cst, *fr)
                g = dve.do(lambda e, ps=ps, j=j: e.tensor_tensor(
                    run[:, 1, j, :], ps[:, :], run[:, 1, j, :], ALU.mult), w, qk[1, j])
                freed[n] = (g,)
                on.append(g)
            den_free[0] = (w,)

        def mixed(c):
            run = runs[c % 2]
            on = shared[c]
            for t in range(4):
                n, ps, fr = bank()
                for j in range(4):
                    w = pe.do(lambda e, ps=ps, j=j, t=t: e.matmul(
                        ps[:, 0:D], run[:, 1, j, t * P:(t + 1) * P], wout[:, j, :],
                        start=(j == 0), stop=(j == 3)), on[j], t_wout, *fr, sig=(j == 3))
                g = dve.do(lambda e, ps=ps, c=c, t=t: e.tensor_tensor(
                    x[:, 4 * c + t, :], ps[:, 0:D], x[:, 4 * c + t, :], ALU.add), w)
                freed[n] = (g,)
            t_x[c] = g
            run_free[c % 2] = (w,)

        kv_done = []

        def keys():
            t_b = dve.do(lambda e: e.tensor_scalar(bq8[:, :], bqk[:, 0, :], 0.125, None, ALU.mult), t_ctx)
            for j in range(8):
                n, ps, fr = bank()
                for k in range(2):
                    w = pe.do(lambda e, ps=ps, k=k, j=j: e.matmul(
                        ps[:, 0:2 * SK], wk[:, k, j * P:(j + 1) * P], ctxT[:, k, :], start=(k == 0), stop=(k == 1)),
                        t_ctx, t_wk, *fr, sig=(k == 1))
                for b in range(B):
                    for r in range(2):
                        half = slice(64 * r, 64 * r + 64)
                        to = kbd[half, b, j, r * SK:(r + 1) * SK]
                        fro = ps[half, b * SK:(b + 1) * SK]
                        by = bqk[half, 1, j:j + 1]
                        if r:
                            t_k2 = dve.do(lambda e, to=to, fro=fro, by=by: e.tensor_scalar(
                                to, fro, by, None, ALU.add), w, t_kz)
                        else:
                            t_k = act.do(lambda e, to=to, fro=fro, by=by: e.activation(
                                to, fro, ACT.Identity, bias=by), w, t_kz)
                freed[n] = (t_k, t_k2)
            kv_done.extend([t_b, t_k, t_k2])

        groups = [(b, t, h) for b in range(B) for t in range(3) for h in range(2)]
        segments = [[(0, 128, 0)], [(0, 32, 0), (32, 64, 1), (64, 128, 1)], [(0, 58, 1)]]

        def contents(count):
            for b, t, h in [groups.pop(0) for _ in range(count)]:
                n, ps, fr = bank()
                for k in range(2):
                    w = pe.do(lambda e, ps=ps, k=k, b=b, t=t, h=h: e.matmul(
                        ps[:, :], ctxV[:, k, b, t, :], wv[:, k, h * 512:(h + 1) * 512],
                        start=(k == 0), stop=(k == 1)), t_ctxV, t_wv, *fr, sig=(k == 1))
                for lo, hi, r in segments[t]:
                    t_v = dve.do(lambda e, ps=ps, b=b, t=t, h=h, lo=lo, hi=hi, r=r: e.tensor_tensor(
                        vbd[lo:hi, b, t, 4 * h:4 * h + 4, 64 * r:64 * r + 64],
                        ps[lo:hi, :].rearrange("p (j r d) -> p j r d", j=4, r=2)[:, :, r, :],
                        bvB[lo:hi, h * 512:(h + 1) * 512].rearrange("p (j r d) -> p j r d", j=4, r=2)[
                            :, :, r, :], ALU.add), w, t_vz)
                freed[n] = (t_v,)
            kv_done[3:] = [t_v, w]

        fs_sem = [sem() for _ in range(2)]
        mk_sem = [sem() for _ in range(2)]
        mk_free = [(), ()]
        fs_free = [(), ()]
        att_free = [()] * 4
        q_free = [()]
        normed = {}
        probs = {}
        sided = {}
        over = {}
        top = {}

        def queries(u, rT):
            r, xT = rT
            c, cols = u // 2, slice(u % 2 * 256, u % 2 * 256 + 256)
            for t in (2 * u, 2 * u + 1):
                a = pool.do(lambda e, t=t: e.tensor_tensor(x[:, t, :], x[:, t, :], boB[:, :], ALU.add), *xT, t_wo)
            normed[u] = (a,)
            for j in range(8):
                n, ps, fr = bank()
                for k in range(2):
                    w = pe.do(lambda e, ps=ps, k=k, j=j: e.matmul(
                        ps[:, 0:256], wq[:, k, j * P:(j + 1) * P], xnT[:, r, k, cols], start=(k == 0), stop=(k == 1)),
                        *xT, t_wq, *fr, sig=(k == 1))
                g = act.do(lambda e, ps=ps, j=j: e.activation(qT[:, j, :], ps[:, 0:256], ACT.Identity,
                                                              bias=bq8[:, j:j + 1], scale=0.125),
                           w, kv_done[0], *q_free[0])
                freed[n] = (g,)
            xnT_free[r] = (w,)
            return (g,)

        def fetch(t):
            s = t % 2
            sp.dma(fs_sem[s], 0, fs[:, s, :, :], A["fside"][t], *fs_free[s])

        def fetch_mask(t):
            s = t % 2
            sp.dma(mk_sem[s], 0, mk[:, s, :, :], A["mask"][t], *mk_free[s])

        def scores(u, tq):
            for t in (2 * u, 2 * u + 1):
                b, s, a4 = t // 8, t % 2, t % 4
                tf = (fs_sem[s], 16 * (t // 2 + 1))
                for j in range(8):
                    n, ps, fr = bank()
                    w = pe.do(lambda e, ps=ps, j=j, b=b, t=t: e.matmul(
                        ps[:, 0:PW], qT[:, j, (t % 2) * P:(t % 2 + 1) * P], kbd[:, b, j, :], start=True, stop=True),
                        *tq, kv_done[1], kv_done[2], *fr)
                    g = dve.do(lambda e, ps=ps, j=j, s=s, a4=a4: e.tensor_tensor(
                        att[:, a4, 2 * j:2 * j + 2, 0:SK],
                        ps[:, 0:PW].rearrange("p (r k) -> p r k", r=2),
                        fs[:, s, 2 * j:2 * j + 2, :], ALU.mult), w, tf, *att_free[a4])
                    freed[n] = (g,)
                q_free[0] = (w,)
                sided[t] = g

        def masked(t):
            s, a4 = t % 2, t % 4
            over[t] = dve.do(lambda e: e.scalar_tensor_tensor(
                out=att[:, a4, :, 0:SK], in0=mk[:, s, :, :], scalar=-BIG, in1=att[:, a4, :, 0:SK],
                op0=ALU.mult, op1=ALU.add), sided[t], (mk_sem[s], 16 * (t // 2 + 1)))
            fs_free[s] = (sided[t],)
            mk_free[s] = (over[t],)
            if t + 2 < NT:
                fetch(t + 2)
                fetch_mask(t + 2)

        def topped(t):
            a4 = t % 4
            g = dve.do(lambda e: e.tensor_reduce(mx[:, a4, 0, :], att[:, a4, :, 0:SK], AX.X, ALU.max), over[t])
            g = dve.do(lambda e: e.tensor_scalar(mx[:, a4, 1, :], mx[:, a4, 0, :], -1.0e38, -BIG,
                                                 ALU.is_le, ALU.mult), g)
            top[t] = dve.do(lambda e: e.scalar_tensor_tensor(
                out=mx[:, a4, 1, :], in0=mx[:, a4, 1, :], scalar=BIG, in1=mx[:, a4, 0, :],
                op0=ALU.mult, op1=ALU.subtract), g)

        def raised(t, heads):
            a4 = t % 4
            for h in heads:
                probs[t] = act.do(lambda e, h=h: e.activation(
                    att[:, a4, h, 0:SK], att[:, a4, h, 0:SK], ACT.Exp,
                    bias=mx[:, a4, 1, h:h + 1], accum_out=mx[:, a4, 2, h:h + 1]), top[t])

        def scaled(t):
            a4 = t % 4
            e1 = probs[t]
            g = dve.do(lambda e: e.reciprocal(mx[:, a4, 3, :], mx[:, a4, 2, :]), e1)
            probs[t] = pool.do(lambda e: e.tensor_tensor(
                att[:, a4, :, 0:SK], att[:, a4, :, 0:SK],
                mx[:, a4, 3, :].rearrange("p (h a) -> p h a", a=1).broadcast_to([P, H, SK]), ALU.mult), g, e1)

        def softmax(u, more):
            t0, t1 = 2 * u, 2 * u + 1
            masked(t0)
            topped(t0)
            return [lambda: None,
                    lambda: (masked(t1), topped(t1), raised(t0, range(0, 5))),
                    lambda: raised(t0, range(5, 11)),
                    lambda: raised(t0, range(11, 16)),
                    lambda: (more(), scaled(t0), raised(t1, range(0, 8))),
                    lambda: (raised(t1, range(8, 16)), scaled(t1))]

        pT_free = [(), ()]
        oT_free = [()]

        def values(u, between):
            b = u // 4
            oc = []
            pend = None

            def product(jj, s, ev):
                n, ps, fr = bank()
                for i in range(2):
                    for tt, m in enumerate([128, 128, 58]):
                        w2 = pe.do(lambda e, ps=ps, i=i, tt=tt, m=m, jj=jj, s=s: e.matmul(
                            ps[:, i * 256:(i + 1) * 256], vbd[0:m, b, tt, 2 * jj + i, :], pT[0:m, s, i, tt, :],
                            start=(tt == 0), stop=(tt == 2)), *ev, kv_done[3], *fr, sig=(tt == 2))
                pT_free[s] = (w2,)
                g = dve.do(lambda e, ps=ps, jj=jj: e.tensor_copy(
                    oT[:, 2 * jj:2 * jj + 2, :], ps[:, :].rearrange("p (i q) -> p i q", i=2)), w2, *oT_free[0])
                freed[n] = (g,)
                oc.append(g)

            for jj in range(4):
                s = jj % 2
                ev = []
                n2, ps2, fr2 = bank()
                for i in range(2):
                    j = 2 * jj + i
                    n, ps, fr = bank()
                    for tt, (lo, m) in enumerate([(0, 128), (128, 128), (256, 58)]):
                        for q in range(2):
                            a4 = (2 * u + q) % 4
                            o = ps[0:m, (2 * tt + q) * P:(2 * tt + q + 1) * P] if tt < 2 else \
                                ps2[0:m, (2 * i + q) * P:(2 * i + q + 1) * P]
                            w = pe.do(lambda e, o=o, a4=a4, j=j, lo=lo, m=m: e.transpose(
                                o, att[:, a4, 2 * j:2 * j + 2, :].rearrange("p r k -> p (r k)")[:, lo:lo + m],
                                ident[:, :]), probs[2 * u + q], *fr, *fr2, sig=(q == 1))
                        if tt == 1:
                            g = act.do(lambda e, ps=ps, s=s, i=i: e.copy(
                                pT[:, s, i, 0:2, :], ps[:, :].rearrange("p (t q) -> p t q", t=2)), w, *pT_free[s])
                            freed[n] = (g,)
                            ev.append(g)
                g = act.do(lambda e, ps2=ps2, s=s: e.copy(
                    pT[0:58, s, :, 2, :], ps2[0:58, :].rearrange("p (i q) -> p i q", i=2)), w, *pT_free[s])
                freed[n2] = (g,)
                ev.append(g)
                if pend:
                    product(*pend)
                pend = (jj, s, ev)
                if between:
                    between.pop(0)()
            for q in range(2):
                att_free[(2 * u + q) % 4] = (w,)
            product(*pend)
            if between:
                between.pop(0)()
            for q in range(2):
                t = 2 * u + q
                n, ps, fr = bank()
                for j in range(8):
                    w = pe.do(lambda e, ps=ps, j=j, q=q: e.matmul(
                        ps[:, 0:D], oT[:, j, q * P:(q + 1) * P], wo[:, j, :], start=(j == 0), stop=(j == 7)),
                        oc[j // 2], t_wo, *fr, sig=(j == 7))
                g = dve.do(lambda e, ps=ps, t=t: e.tensor_tensor(x[:, t, :], ps[:, 0:D], x[:, t, :], ALU.add),
                           w, *normed[u])
                freed[n] = (g,)
            oT_free[0] = (w,)
            t_x[u // 2] = g
            for part in between:
                part()

        def per_token(v):
            return v.rearrange("p (t a) -> p t a", a=1).broadcast_to([P, 4, NE])

        def per_expert(v):
            return v.rearrange("p (a n) -> p a n", a=1).broadcast_to([P, 4, NE])

        def dstep(fn, *waits):
            return dve.do(fn, (dve.sem, dve.count), *waits)

        x3 = {}
        n3 = {}
        added = {}
        gate_done = {}

        def third(c):
            a = n3[c]
            x3[c] = turned(a)
            for t in range(4 * c, 4 * c + 4):
                a2 = pool.do(lambda e, t=t: e.tensor_tensor(x[:, t, :], x[:, t, :], sb2B, ALU.add), a, t_s2)
            added[c] = (a2,)

        def gate(c):
            r, xT = x3[c]
            n, ps, fr = bank()
            for i in range(4):
                for k in range(2):
                    w = pe.do(lambda e, ps=ps, k=k, i=i: e.matmul(
                        ps[:, NE * i:NE * i + NE], xnT[:, r, k, i * P:(i + 1) * P], gw[:, k, :],
                        start=(k == 0), stop=(k == 1)), *xT, t_sm, *fr, sig=(k == 1))
            p1, p2 = o1[:, 4 * c:4 * c + 4, :], o2[:, 4 * c:4 * c + 4, :]
            lg4 = ps[:, 0:4 * NE].rearrange("p (t n) -> p t n", t=4)
            ids = dve.do(lambda e: e.tensor_copy(xn[:, :, D].bitcast(I32), tokid[:, 4 * c:4 * c + 4, 0]),
                         t_sm, *xn_scattered[0])
            dstep(lambda e: e.tensor_reduce(gm[:, :], lg4, AX.X, ALU.max), w)
            g = dstep(lambda e: e.tensor_tensor(lg[:, :, :], lg4, per_token(gm[:, :]), ALU.subtract))
            freed[n] = (g,)
            w = act.do(lambda e: e.activation(lg[:, :, :], lg[:, :, :], ACT.Exp), g)
            dstep(lambda e: e.tensor_reduce(gm[:, :], lg[:, :, :], AX.X, ALU.add), w)
            dstep(lambda e: e.reciprocal(gm[:, :], gm[:, :]))
            dstep(lambda e: e.tensor_tensor(lg[:, :, :], lg[:, :, :], per_token(gm[:, :]), ALU.mult))
            dstep(lambda e: e.tensor_tensor(ga[:, :, :], lg[:, :, :], per_expert(gbB[:, :]), ALU.add))
            for i, o in enumerate((p1, p2)):
                dstep(lambda e: e.tensor_reduce(gm[:, :], ga[:, :, :], AX.X, ALU.max))
                dstep(lambda e: e.tensor_tensor(gt[:, :, :], ga[:, :, :], per_token(gm[:, :]), ALU.is_ge))
                dstep(lambda e: e.tensor_tensor(gt[:, :, :], gt[:, :, :], per_expert(iot[:, :]), ALU.mult))
                dstep(lambda e: e.tensor_reduce(gm[:, :], gt[:, :, :], AX.X, ALU.max))
                dstep(lambda e, o=o: e.tensor_tensor(o, per_expert(iot[:, :]), per_token(gm[:, :]), ALU.is_equal))
                dstep(lambda e, o=o: e.tensor_tensor(gt[:, :, :], o, lg[:, :, :], ALU.mult))
                dstep(lambda e, i=i: e.tensor_reduce(wsel[:, i, 4 * c:4 * c + 4], gt[:, :, :], AX.X, ALU.add))
                if i == 0:
                    dstep(lambda e, o=o: e.scalar_tensor_tensor(
                        out=ga[:, :, :], in0=o, scalar=-BIG, in1=ga[:, :, :], op0=ALU.mult, op1=ALU.add))
            g = dstep(lambda e: e.tensor_tensor(gt[:, :, :], p1, p2, ALU.add))
            gate_done[c] = (g, ids)

        xn_scattered = [()]

        def placed(c):
            g, ids = gate_done[c]
            n, ps, fr = bank()
            gt2 = gt[:, :, :].rearrange("p t n -> p (t n)")
            pe.do(lambda e, ps=ps: e.matmul(ps[:, 0:32], tri, gt2, start=True, stop=True),
                  g, t_s2, *fr, sig=False)
            w = pe.do(lambda e, ps=ps: e.matmul(ps[:, 32:64], ones[:, :], gt2, start=True, stop=True), t_on)
            dstep(lambda e: e.tensor_copy(cnt[:, 0, :], cnt[:, 4, :]), t_c0)
            for i in range(4):
                dstep(lambda e, i=i, ps=ps: e.tensor_tensor(
                    cnt[:, i + 1, :], ps[:, 32 + NE * i:32 + NE * i + NE], cnt[:, i, :], ALU.add), w)
            p4 = ps[:, 0:32].rearrange("p (t n) -> p t n", t=4)
            g = dstep(lambda e, p4=p4: e.tensor_tensor(ga[:, :, :], p4, cnt[:, 0:4, :], ALU.add))
            freed[n] = (g,)
            dstep(lambda e: e.tensor_tensor(ga[:, :, :], ga[:, :, :], per_expert(eoff[:, :]), ALU.add))
            for i, o in enumerate((o1, o2)):
                dstep(lambda e, o=o: e.tensor_tensor(gt[:, :, :], ga[:, :, :], o[:, 4 * c:4 * c + 4, :], ALU.mult))
                dstep(lambda e, i=i: e.tensor_reduce(posf[:, i, :], gt[:, :, :], AX.X, ALU.add))
            g = dstep(lambda e: e.tensor_copy(pos[:, c, :, :], posf[:, :, :]))
            for k in range(2):
                if k == 1:
                    ids = pool.do(lambda e: e.tensor_copy(xn[:, :, D].bitcast(I32), tokid[:, 4 * c:4 * c + 4, 1]),
                                 (xs_sem, xs_total[0]))
                xs_total[0] += 64
                for i in range(4):
                    pool.items.append(((g, ids), lambda e, i=i, k=k: e.indirect_dma_start(
                        out=xs, out_offset=bass.IndirectOffsetOnAxis(
                            ap=pos[:, c, k, i:i + 1].bitcast(U32), axis=0),
                        in_=xn[:, i, :], in_offset=None).then_inc(xs_sem, 16), False))
            xn_scattered[0] = ((xs_sem, xs_total[0]),)
            xn_free[0] += xn_scattered[0]

        hA_free = [(), ()]
        hZ_free = [(), ()]
        part = {}

        def shared_in(c, half):
            r, xT = x3[c]
            cols = slice(half * 256, half * 256 + 256)
            zt = []
            for m, (lo, mw) in enumerate(MT):
                n, ps, fr = bank()
                for q, wm in enumerate((sw1, sw3)):
                    for k in range(2):
                        w = pe.do(lambda e, ps=ps, k=k, wm=wm, lo=lo, mw=mw, q=q: e.matmul(
                            ps[0:mw, q * 256:q * 256 + 256], wm[:, k, lo:lo + mw], xnT[:, r, k, cols],
                            start=(k == 0), stop=(k == 1)), *xT, t_sm, *fr, sig=(q == 1 and k == 1))
                a = act.do(lambda e, ps=ps, m=m, mw=mw: e.activation(
                    hA[0:mw, :], ps[0:mw, 0:256], ACT.Identity, bias=b13[0:mw, 0, m:m + 1]), w, *hA_free[0])
                g = dve.do(lambda e, ps=ps, m=m, mw=mw: e.scalar_tensor_tensor(
                    out=hZ[0:mw, m, :], in0=ps[0:mw, 256:512], scalar=b13[0:mw, 1, m:m + 1],
                    in1=hA[0:mw, :], op0=ALU.add, op1=ALU.mult), a, *hZ_free[0])
                freed[n] = (g,)
                hA_free[0] = (g,)
                zt.append(act.do(lambda e, m=m, mw=mw: e.activation(
                    hZ[0:mw, m, :], hZ[0:mw, m, :], ACT.Silu), g))
            xnT_free[r] = (w,)
            part[c, half] = zt

        def shared_out(c, half):
            zt = part[c, half]
            for i in range(2):
                t = 4 * c + 2 * half + i
                n, ps, fr = bank()
                for m, (lo, mw) in enumerate(MT):
                    w = pe.do(lambda e, ps=ps, m=m, mw=mw, i=i: e.matmul(
                        ps[:, 0:D], hZ[0:mw, m, i * P:(i + 1) * P], sw2[0:mw, m, :],
                        start=(m == 0), stop=(m == 2)), zt[m], *fr, sig=(m == 2))
                g = dve.do(lambda e, ps=ps, t=t: e.tensor_tensor(x[:, t, :], ps[:, 0:D], x[:, t, :], ALU.add),
                           w, *added[c])
                freed[n] = (g,)
                t_x[c] = g
            hZ_free[0] = (w,)

        a = norm(0, (t_x[0],))
        r0 = turned(a)
        keys()
        decays()
        a = norm(1, (t_x[1],))
        scan(0, r0)
        r1 = turned(a)
        a = norm(2, (t_x[2],))
        scan(1, r1)
        r2 = turned(a)
        contents(4)
        summed(0)
        contents(2)
        divided(0)
        summed(1)
        mixed(0)
        a = norm(3, (t_x[3],))
        contents(3)
        divided(1)
        scan(2, r2)
        r3 = turned(a)
        mixed(1)
        summed(2)
        contents(3)
        a = norm(0, (t_x[0],))
        divided(2)
        scan(3, r3)
        rT = turned(a)
        mixed(2)
        a = norm(1, (t_x[1],))
        summed(3)
        early = run_free[0] + chunk_free[0] + tmp_free[0] + tuple(kv_done)
        q_free[0] = early
        tq = queries(0, rT)
        divided(3)
        t_az = pool.do(lambda e: e.memset(att[:, 0:2, :, SK:HK], 0.0), *early)
        att_free[0:2] = [early + (t_az,)] * 2
        fs_free[:] = [early, early]
        mk_free[0] = early
        fetch(0)
        fetch_mask(0)
        fetch(1)
        scores(0, tq)
        mixed(3)
        late = early + run_free[1] + den_free[0]
        t_az = pool.do(lambda e: e.memset(att[:, 2:4, :, SK:HK], 0.0), *late)
        att_free[2:4] = [late + (t_az,)] * 2
        pT_free[:] = [late, late]
        oT_free[0] = late
        mk_free[1] = late
        fetch_mask(1)
        t_s2 = load(sp, [(sb2B, rows(A["L0_ffn_sb2"], D)), (tri, A["tri"])], *late)
        fill = {3: (0, 0), 4: (0, 1), 5: (1, 0), 6: (1, 1), 7: (2, 0)}
        masked(0)
        topped(0)
        rN = turned(a)
        tq = queries(1, rT)
        raised(0, range(H))
        masked(1)
        topped(1)
        raised(1, range(H))
        for u in range(1, 8):
            scores(u, tq)
            if u == 1:
                scaled(0)
                scaled(1)
            if u % 2 == 0 and u < 6:
                rN = turned(a)
            gating = u >= 3 and u % 2 == 1
            values(u - 1, softmax(u, lambda: gate((u - 3) // 2) if gating else None))
            if u >= 3 and u % 2 == 1:
                placed((u - 3) // 2)
            if u % 2 == 0:
                n3[u // 2 - 1] = norm(u // 2 - 1, (t_x[u // 2 - 1],))
            if u in fill:
                shared_in(*fill[u])
            if u % 2 == 1:
                rT = rN
            if u < 7:
                tq = queries(u + 1, rT)
            if u in fill:
                shared_out(*fill[u])
            if u % 2 == 0:
                third(u // 2 - 1)
            if u in (1, 3):
                a = norm(u // 2 + 2, (t_x[u // 2 + 2],))
        t_r3 = mk_free[0] + mk_free[1]
        values(7, [])
        n3[3] = norm(3, (t_x[3],))
        shared_in(2, 1)
        shared_out(2, 1)
        third(3)
        gate(3)
        shared_in(3, 0)
        placed(3)
        shared_out(3, 0)

        late = att_free[3] + oT_free[0] + pT_free[0] + pT_free[1]
        ew_sem, ew2_sem = sem(), sem()
        for ex in range(NE):
            d = ew2_sem
            sp.dma(d, 0, ew2[:, ex * 768:ex * 768 + 512].rearrange("p (k n) -> p k n", k=2),
                   A["L0_ffn_w2"][ex, 0:256].rearrange("(k p) n -> p k n", p=P), *t_r3)
            sp.dma(d, 0, ew2[0:96, ex * 768 + 512:ex * 768 + 768], A["L0_ffn_w2"][ex, 256:352])
        t_ew2 = (ew2_sem, 256)
        sp.dma(ew_sem, 0, eb, A["ebias"].broadcast_to([P, NE * 960]), *late)
        for ex in range(NE):
            for q, wm in enumerate(("L0_ffn_w1", "L0_ffn_w3")):
                sp.dma(ew_sem, 0, ew13[:, ex * 1408 + q * 704:ex * 1408 + q * 704 + 704].rearrange(
                    "p (k n) -> p k n", k=2), A[wm][ex].rearrange("(k p) n -> p k n", p=P))
        t_ew = (ew_sem, 272)

        n_e = cnt[:, 4, :]
        dstep(lambda e: e.tensor_tensor(ntf[:, :], n_e, eoff[:, :], ALU.add))
        t_pr = dstep(lambda e: e.tensor_copy(prow[:, :], ntf[:, :]))
        dstep(lambda e: e.tensor_scalar(ntf[:, :], n_e, 127.0, None, ALU.add))
        dstep(lambda e: e.tensor_copy(nti[:, :], ntf[:, :]))
        dstep(lambda e: e.tensor_single_scalar(nti[:, :], nti[:, :], 7, ALU.logical_shift_right))
        dstep(lambda e: e.tensor_copy(ntf[:, :], nti[:, :]))
        dstep(lambda e: e.tensor_tensor_scan(end[:, :], ones[:, 0:NE], ntf[:, :], 0.0, ALU.mult, ALU.add))

        def by_slot(v):
            return v.rearrange("p (s a) -> p s a", a=1).broadcast_to([P, NS, NE])

        def by_end(v):
            return v.rearrange("p (a n) -> p a n", a=1).broadcast_to([P, NS, NE])

        dstep(lambda e: e.tensor_tensor(cmp_[:, :, :], by_slot(slot[:, :]), by_end(end[:, :]), ALU.is_ge))
        dstep(lambda e: e.tensor_reduce(se[:, 0, :], cmp_[:, :, :], AX.X, ALU.add))
        dstep(lambda e: e.tensor_tensor(cmp_[:, :, :], cmp_[:, :, :], by_end(end[:, :]), ALU.mult))
        dstep(lambda e: e.tensor_reduce(se[:, 1, :], cmp_[:, :, :], AX.X, ALU.max))
        dstep(lambda e: e.tensor_tensor(se[:, 1, :], slot[:, :], se[:, 1, :], ALU.subtract))
        dstep(lambda e: e.tensor_scalar(se[:, 1, :], se[:, 1, :], float(P), None, ALU.mult))
        dstep(lambda e: e.scalar_tensor_tensor(out=se[:, 1, :], in0=se[:, 0, :], scalar=float(RG), in1=se[:, 1, :],
                                               op0=ALU.mult, op1=ALU.add))
        dstep(lambda e: e.tensor_scalar(se[:, 0, :], se[:, 0, :], float(NE - 1), None, ALU.min))
        t_sl = dstep(lambda e: e.tensor_copy(sei[:, :, :], se[:, 0:2, :]))

        shared_in(3, 1)
        shared_out(3, 1)

        def pad(ex):
            def go(e):
                v = e.value_load(prow[0:1, ex:ex + 1], min_val=ex * RG, max_val=ex * RG + N)
                return e.dma_start(xs[bass.ds(v, P), :], A["pad"][ex * P:(ex + 1) * P, :]).then_inc(xp_sem, 16)
            return go

        for ex in range(NE):
            sp.items.append(((t_pr,), pad(ex), False))
        t_xs = (xs_sem, xs_total[0])
        t_xp = (xp_sem, 16 + 16 * NE)

        xl_sem = [sem() for _ in range(6)]
        zr_sem = [sem() for _ in range(4)]
        xsl_free = [late] * 6
        xsT_free = [late] * 2
        sA_free = [late] * 2
        sT_free = [late] * 2
        sY_free = [late] * 4
        w_reg, b_reg = {}, {}
        flip, hid, hidT = {}, {}, {}

        def read(s):
            def go(e):
                v = e.value_load(sei[0:1, 1, s:s + 1], min_val=0, max_val=XROWS - P)
                return e.dma_start(xsl[:, s % 6, :], xs[bass.ds(v, P), :]).then_inc(xl_sem[s % 6], 16)
            sp.items.append(((t_sl, t_xs, t_xp, *xsl_free[s % 6]), go, False))

        def rows_turned(s):
            i2 = s % 2
            n, ps, fr = bank()
            for k in range(2):
                w = pe.do(lambda e, ps=ps, k=k: e.transpose(ps[:, k * P:(k + 1) * P],
                                                            xsl[:, s % 6, k * P:(k + 1) * P], ident[:, :]),
                          (xl_sem[s % 6], 16 * (s // 6 + 1)), *fr, sig=(k == 1))
            g = act.do(lambda e, ps=ps: e.copy(xsT[:, i2, :, :], ps[:, 0:256].rearrange("p (k q) -> p k q", k=2)),
                       w, *xsT_free[i2])
            freed[n] = (g,)
            flip[s] = g

        def hidden(s):
            i2 = s % 2

            def pick(e):
                w_reg[s] = e.value_load(sei[0:1, 0, s:s + 1], min_val=0, max_val=NE - 1)

            def pickb(e):
                b_reg[s] = e.value_load(sei[0:1, 0, s:s + 1], min_val=0, max_val=NE - 1)

            pe.items.append(((t_sl,), pick, False))
            dve.items.append(((t_sl,), pickb, False))
            ws = []
            for q in range(2):
                n, ps, fr = bank()
                for k in range(2):
                    w = pe.do(lambda e, ps=ps, k=k, q=q: e.matmul(
                        ps[:, 0:F], xsT[:, i2, k, :], ew13[:, bass.ds(w_reg[s] * 1408 + q * 704 + k * F, F)],
                        start=(k == 0), stop=(k == 1)), flip[s], t_ew, *fr, sig=(k == 1))
                ws.append((n, ps, w))
            xsT_free[i2] = (w,)
            n, ps, w = ws[0]
            a = dve.do(lambda e, ps=ps: e.tensor_tensor(sA[:, i2, :], ps[:, 0:F], eb[:, bass.ds(b_reg[s] * 960, F)],
                                                        ALU.add), w, t_ew, *sA_free[i2])
            freed[n] = (a,)
            n, ps, w = ws[1]
            z = dve.do(lambda e, ps=ps: e.tensor_tensor(sZ[:, i2, :], ps[:, 0:F],
                                                        eb[:, bass.ds(b_reg[s] * 960 + F, F)], ALU.add), w)
            freed[n] = (z,)
            z = dve.do(lambda e: e.tensor_tensor(sZ[:, i2, :], sZ[:, i2, :], sA[:, i2, :], ALU.mult), a, z)
            hid[s] = act.do(lambda e: e.activation(sZ[:, i2, :], sZ[:, i2, :], ACT.Silu), z)

        def hidden_turned(s):
            i2 = s % 2
            n, ps, fr = bank()
            for m, (lo, mw) in enumerate(MT):
                w = pe.do(lambda e, ps=ps, m=m, lo=lo, mw=mw: e.transpose(
                    ps[0:mw, m * P:(m + 1) * P], sZ[:, i2, lo:lo + mw], ident[:, :]), hid[s], *fr, sig=(m == 2))
            sA_free[i2] = (w,)
            act.do(lambda e, ps=ps: e.copy(sT[:, i2, 0:2, :], ps[:, 0:256].rearrange("p (m q) -> p m q", m=2)),
                   w, *sT_free[i2])
            g = act.do(lambda e, ps=ps: e.copy(sT[0:96, i2, 2, :], ps[0:96, 256:384]))
            freed[n] = (g,)
            hidT[s] = g

        def results(s):
            i2 = s % 2
            n, ps, fr = bank()
            for m, (lo, mw) in enumerate(MT):
                w = pe.do(lambda e, ps=ps, m=m, mw=mw: e.matmul(
                    ps[:, 0:D], sT[0:mw, i2, m, :], ew2[0:mw, bass.ds(w_reg[s] * 768 + m * D, D)],
                    start=(m == 0), stop=(m == 2)), hidT[s], t_ew2, *fr, sig=(m == 2))
            sT_free[i2] = (w,)
            g = dve.do(lambda e, ps=ps: e.tensor_tensor(sY[:, s % 4, :], ps[:, 0:D],
                                                        eb[:, bass.ds(b_reg[s] * 960 + 2 * F, D)], ALU.add),
                       w, *sY_free[s % 4])
            freed[n] = (g,)
            pool.items.append(((g,), lambda e: e.indirect_dma_start(
                out=zs, out_offset=bass.IndirectOffsetOnAxis(ap=xsl[:, s % 6, D:D + 1].bitcast(U32), axis=0),
                in_=sY[:, s % 4, :], in_offset=None).then_inc(zr_sem[s % 4], 16), False))
            done = (zr_sem[s % 4], 16 * (s // 4 + 1))
            sY_free[s % 4] = (done,)
            xsl_free[s % 6] = (done,)
            return w

        for s in range(4):
            read(s)
        rows_turned(0)
        for s in range(NS + 2):
            if s + 1 < NS:
                rows_turned(s + 1)
            if s < NS:
                hidden(s)
            if 1 <= s <= NS:
                hidden_turned(s - 1)
            if s >= 2:
                w = results(s - 2)
            if s + 4 < NS:
                read(s + 4)
        all_z = tuple((zr_sem[i], 16 * len(range(i, NS, 4))) for i in range(4))

        zv = zs[0:2 * N, :].rearrange("(w c t p) n -> p c w t n", w=2, c=NCH, p=P)
        o_sem = sem()
        for c in range(NCH):
            zc = sem()
            for k in range(2):
                sp.dma(zc, 32, zb[:, c, k, :, :], zv[:, c, k, :, :], w, *all_z)
            for i in range(4):
                t = 4 * c + i
                for k in range(2):
                    g = dve.do(lambda e, t=t, k=k, i=i, c=c: e.scalar_tensor_tensor(
                        out=x[:, t, :], in0=zb[:, c, k, i, :], scalar=wsel[:, k, t:t + 1], in1=x[:, t, :],
                        op0=ALU.mult, op1=ALU.add), (zc, 32), *([(dve.sem, dve.count)] if k else [t_x[c]]))
            act.dma(o_sem, 0, outv[:, 4 * c:4 * c + 4, :], x[:, 4 * c:4 * c + 4, :], g)
        act.wait((o_sem, 16 * NCH))

        block = ctx.enter_context(nc.Block())

        @block.sync
        def _(eng):
            sp.play(eng)

        @block.scalar
        def _(eng):
            act.play(eng)

        @block.gpsimd
        def _(eng):
            pool.play(eng)

        @block.vector
        def _(eng):
            dve.play(eng)

        @block.tensor
        def _(eng):
            pe.play(eng)


def layout(inputs):
    a = {k: np.ascontiguousarray(v) for k, v in inputs.items()}
    o = {k: a[k] for k in ("x", "L0_attn_w_qkv", "L0_attn_w_out", "L0_xattn_Wq", "L0_xattn_Wk", "L0_xattn_Wv",
                           "L0_xattn_Wo", "L0_xattn_bv", "L0_xattn_bo", "L0_ffn_gate_b", "L0_ffn_w1", "L0_ffn_w3",
                           "L0_ffn_w2", "L0_ffn_sw1", "L0_ffn_sw3", "L0_ffn_sw2", "L0_ffn_sb2")}
    ctx = a["ctx_1024"]
    o["ctxT"] = np.ascontiguousarray(ctx.reshape(B * SK, D).T)
    cv = np.zeros((D, B, 3, P), ctx.dtype)
    for b in range(B):
        t = ctx[b].T
        cv[:, b, 0, :] = t[:, 0:128]
        cv[:, b, 1, 0:26] = t[:, 128:154]
        cv[:, b, 1, 32:128] = t[:, 0:96]
        cv[:, b, 2, 0:58] = t[:, 96:154]
    o["ctxV"] = cv.reshape(D, B * 3 * P)
    o["fside"] = np.ascontiguousarray(
        a["fside_Bx16xSxS2_0"].reshape(B, H, 8, P, SK).transpose(0, 2, 3, 1, 4)).reshape(NT, P, H, SK)
    o["mask"] = np.ascontiguousarray(
        a["mask_Bx16xSxS2_bk1"].reshape(B, H, 8, P, SK).transpose(0, 2, 3, 1, 4)).reshape(NT, P, H, SK)
    ab = np.stack([a["L0_attn_alpha"], a["L0_attn_beta"]])
    o["decay"] = np.ascontiguousarray(np.repeat(ab, 16, axis=1).reshape(2, 2, P).transpose(2, 0, 1))
    bqk = np.stack([a["L0_xattn_bq"], a["L0_xattn_bk"]])
    o["bqk"] = np.ascontiguousarray(bqk.reshape(2, 8, P).transpose(2, 0, 1))
    o["gateT"] = np.ascontiguousarray(a["L0_ffn_gate_w"].T.reshape(2, P, NE).transpose(1, 0, 2))
    b13 = np.zeros((2, 384), np.float32)
    b13[0, 0:F], b13[1, 0:F] = a["L0_ffn_sb1"], a["L0_ffn_sb3"]
    o["b13"] = np.ascontiguousarray(b13.reshape(2, 3, P).transpose(2, 0, 1))
    sel = np.zeros((P, 4, P), np.float32)
    for j in range(4):
        for p in range(P):
            sel[p, j, 8 * j + p // 16::32] = 1.0
    o["sel"] = sel
    o["selT"] = np.ascontiguousarray(sel.transpose(2, 1, 0)) * np.float32(0.25)
    o["ident"] = np.eye(P, dtype=np.float32)
    o["cst"] = np.full((P, 2), 1e-5, np.float32)
    o["tri"] = np.triu(np.ones((P, P), np.float32), 1)
    o["eoff"] = np.tile(np.arange(NE).astype(np.float32) * RG, (P, 1))
    o["slot"] = np.tile(np.arange(NS).astype(np.float32), (P, 1))
    tok = np.arange(N, dtype=np.int32).reshape(NT, P).T
    o["tokid"] = np.ascontiguousarray(np.stack([tok, tok + N], 2))
    pad = np.zeros((15 * P, XW), np.float32)
    pad.view(np.int32)[:, D] = 2 * N + np.arange(15 * P, dtype=np.int32)
    o["pad"] = pad
    bias = np.zeros((NE, 960), np.float32)
    bias[:, 0:F], bias[:, F:2 * F], bias[:, 2 * F:] = a["L0_ffn_b1"], a["L0_ffn_b3"], a["L0_ffn_b2"]
    o["ebias"] = bias.reshape(1, NE * 960)
    o["iota"] = np.tile(np.arange(8, 0, -1).astype(np.float32), (P, 1))
    return o


def kernel(**inputs):
    import concourse.bacc as _bacc
    from concourse.bass_utils import run_bass_kernel_spmd as _run

    nc = _bacc.Bacc("TRN2", target_bir_lowering=False, num_devices=1)
    arrays, aps = {}, {}
    for name, a in layout(inputs).items():
        arrays[f"in_{name}_dram"] = a
        aps[name] = nc.dram_tensor(f"in_{name}_dram", a.shape, mybir.dt.from_np(a.dtype), kind="ExternalInput").ap()
    out = nc.dram_tensor("out_0_dram", (B, S, D), F32, kind="ExternalOutput").ap()
    xs = nc.dram_tensor("xs_dram", (XROWS, XW), F32, kind="Internal").ap()
    zs = nc.dram_tensor("zs_dram", (ZROWS, D), F32, kind="Internal").ap()
    decoder(nc, aps, xs, zs, out)
    r = _run(nc, [arrays], core_ids=[0])
    return r.results[0]["out_0_dram"]
```

```python
from contextlib import ExitStack

import numpy as np
import concourse.bass as bass
from concourse import mybir

ALU = mybir.AluOpType
ACT = mybir.ActivationFunctionType
AX = mybir.AxisListType
F32 = mybir.dt.float32
U8 = mybir.dt.uint8
I32 = mybir.dt.int32
U32 = mybir.dt.uint32

P = 128
B = 2
S = 1024
D = 256
N = B * S
NT = N // P
NCH = 4
CT = 512
H = 16
SK = 154
HK = 160
PW = 2 * SK
NE = 8
F = 352
MT = [(0, 128), (128, 128), (256, 96)]
BIG = 3.0e38
RG = 17 * P
NS = (2 * N + NE * (P - 1)) // P
XW = D + 2
XROWS = NE * RG + 7 * P
ZROWS = N + NE * P + 7 * P


class Engine:

    def __init__(self, sem):
        self.sem, self.count, self.items = sem, 0, []

    def do(self, fn, *waits, sig=True):
        self.items.append((waits, fn, sig))
        self.count += sig
        return (self.sem, self.count)

    def dma(self, sem, total, out, in_, *waits):
        self.items.append((waits, lambda e: e.dma_start(out, in_).then_inc(sem, 16), False))
        return (sem, total)

    def wait(self, *waits):
        self.items.append((waits, None, False))

    def play(self, eng):
        seen = {}
        for waits, fn, sig in self.items:
            for sem, value in waits:
                if seen.get(id(sem), 0) < value:
                    eng.wait_ge(sem, value)
                    seen[id(sem)] = value
            if fn is not None:
                ins = fn(eng)
                if sig:
                    ins.then_inc(self.sem, 1)


def decoder(nc, A, xs, zs, out):
    with ExitStack() as ctx:
        def sb(name, shape, dt=F32):
            return ctx.enter_context(nc.sbuf_tensor(name, shape, dt))

        sems = [0]

        def sem():
            sems[0] += 1
            return ctx.enter_context(nc.semaphore(f"s{sems[0]}"))

        pe, dve, act, pool, sp = (Engine(sem()) for _ in range(5))
        banks = [ctx.enter_context(nc.psum_tensor(f"bank{i}", [P, 512], F32)) for i in range(8)]
        freed = [()] * 8
        turn = [0]

        def bank():
            i = turn[0] % 8
            turn[0] += 1
            return i, banks[i], freed[i]

        x = sb("x", [P, NT, D])
        ident = sb("ident", [P, P])
        ones = sb("ones", [P, P])
        cst = sb("cst", [P, 2])
        xn = sb("xn", [P, 4, XW])
        xnT = sb("xnT", [P, 3, 2, CT])
        st = sb("st", [P, 4, 6])
        mv = sb("mv", [P, 4, 2])
        sd = sb("sd", [P, 4])
        rs = sb("rs", [P, 4])
        dec = sb("dec", [P, 2, 2])
        dec2 = sb("dec2", [P, 2, 2])
        carry = sb("carry", [P, 2, 8])
        wq = sb("wq", [P, 2, 1024])
        wo = sb("wo", [P, 8, D])
        bqk = sb("bqk", [P, 2, 8])
        bq8 = sb("bq8", [P, 8])
        boB = sb("boB", [P, D])
        mx = sb("mx", [P, 4, 4, H])
        gw = sb("gw", [P, 2, NE])
        gbB = sb("gbB", [P, NE])
        iot = sb("iot", [P, NE])
        eoff = sb("eoff", [P, NE])
        slot = sb("slot", [P, NS])
        tokid = sb("tokid", [P, NT], I32)
        b13 = sb("b13", [P, 2, 3])
        sw1 = sb("sw1", [P, 2, F])
        sw3 = sb("sw3", [P, 2, F])
        sw2 = sb("sw2", [P, 3, D])
        hA = sb("hA", [P, 256])
        hZ = sb("hZ", [P, 3, 256])
        lg = sb("lg", [P, 4, NE])
        ga = sb("ga", [P, 4, NE])
        gm = sb("gm", [P, 4])
        o1 = sb("o1", [P, NT, NE])
        o2 = sb("o2", [P, NT, NE])
        gt = sb("gt", [P, 4, NE])
        cnt = sb("cnt", [P, 5, NE])
        posf = sb("posf", [P, 2, 4])
        pos = sb("pos", [P, NCH, 2, 4], I32)
        wsel = sb("wsel", [P, 2, 4])
        nti = sb("nti", [P, NE], I32)
        ntf = sb("ntf", [P, NE])
        end = sb("end", [P, NE])
        sei = sb("sei", [P, 2, NS], I32)
        prow = sb("prow", [P, NE], I32)
        KV = sb("KV", [P, 2 * 8 * PW + 2 * 3 * 8 * P])
        kbd = KV[:, 0:4928].rearrange("p (b j n) -> p b j n", b=B, j=8)
        vbd = KV[:, 4928:11072].rearrange("p (b g i n) -> p b g i n", b=B, g=4, i=6)
        eb = KV[:, 0:NE * 960]
        R3 = sb("R3", [P, 6544])
        wqkv = R3[:, 0:1536].rearrange("p (k n) -> p k n", k=2)
        wk = R3[:, 1536:3584].rearrange("p (k n) -> p k n", k=2)
        wv = R3[:, 3584:5632].rearrange("p (k n) -> p k n", k=2)
        fs = R3[:, 0:2 * 2464].rearrange("p (s h k) -> p s h k", s=2, h=H)
        mk = R3[:, 4928:4928 + 2 * 616].bitcast(U8).rearrange("p (s h k) -> p s h k", s=2, h=H)
        sb2B = R3[:, 6160:6416]
        tri = R3[:, 6416:6544]
        ew2 = R3[:, 0:NE * 768]
        wout = sb("wout", [P, 4, D])
        R2 = sb("R2", [P, 5120])
        ctxT = R2[:, 0:616].rearrange("p (k n) -> p k n", k=2)
        ctxV = R2[:, 616:3176].rearrange("p (k b t n) -> p k b t n", k=2, b=B, t=5)
        bvB = R2[:, 3176:4200]
        sel = R2[:, 4200:4712].rearrange("p (j n) -> p j n", j=4)
        selT = hZ[:, 0:2, :].rearrange("p m n -> p (m n)").rearrange("p (j n) -> p j n", j=4)
        pT = R2[:, 0:2560].rearrange("p (s t q) -> p s t q", s=2, t=5)
        oT = R2[:, 3072:5120].rearrange("p (j q) -> p j q", j=8)
        xsl = R2[:, 0:6 * XW].rearrange("p (s n) -> p s n", s=6)
        xsT = R2[:, 1548:2060].rearrange("p (s k q) -> p s k q", s=2, k=2)
        sA = R2[:, 2060:2764].rearrange("p (s n) -> p s n", s=2)
        sZ = R2[:, 2764:3468].rearrange("p (s n) -> p s n", s=2)
        sT = R2[:, 3468:4236].rearrange("p (s m q) -> p s m q", s=2, m=3)
        cmp_ = R2[:, 4236:4236 + NS * NE].rearrange("p (s n) -> p s n", s=NS)
        se = R2[:, 4548:4548 + 2 * NS].rearrange("p (i s) -> p i s", i=2)
        R1 = sb("R1", [P, 12288])
        qb = R1[:, 0:1024].rearrange("p (k n) -> p k n", k=2)
        kb = R1[:, 1024:2048].rearrange("p (k n) -> p k n", k=2)
        kvb = R1[:, 2048:3072].rearrange("p (k n) -> p k n", k=2)
        runs = [R1[:, a:a + 4096].rearrange("p (w j n) -> p w j n", w=2, j=4) for a in (3072, 8192)]
        tmp = R1[:, 7168:8192]
        den = R3[:, 5632:6144]
        qT = R1[:, 0:2048].rearrange("p (j n) -> p j n", j=8)
        att = R1[:, 2048:12288].rearrange("p (s h k) -> p s h k", s=4, h=H)
        ew13 = R1[:, 0:NE * 1408]
        sY = R1[:, 11264:12288].rearrange("p (s n) -> p s n", s=4)

        def load(q, parts, *waits):
            s = sem()
            total = 16 * len(parts)
            for o, i in parts:
                q.dma(s, total, o, i, *waits)
            return (s, total)

        def rows(v, n):
            return v.rearrange("(a n) -> a n", a=1).broadcast_to([P, n])

        xv = A["x"].rearrange("b (t p) d -> p (b t) d", p=P)
        t_id = load(act, [(ident[:, :], A["ident"]), (cst[:, :], A["cst"])])
        t_ctx = load(act, [(ctxT, A["ctxT"].rearrange("(k p) n -> p k n", p=P)),
                           (bqk[:, :, :], A["bqk"])])
        t_x = [load(sp, [(x[:, i:i + 2, :], xv[:, i:i + 2, :]) for i in (0, 2)])]
        t_wk = load(sp, [(wk, A["L0_xattn_Wk"].rearrange("(k p) n -> p k n", p=P))])
        t_wqkv = load(sp, [(wqkv, A["L0_attn_w_qkv"].rearrange("(k p) n -> p k n", p=P))])
        t_cst = load(act, [(dec[:, :, :], A["decay"]), (sel, A["sel"]), (selT, A["selT"])])
        for c in range(1, NCH):
            t_x.append(load(sp, [(x[:, 4 * c:4 * c + 4, :], xv[:, 4 * c:4 * c + 4, :])]))
        t_ctxV = load(act, [(R2[:, 616:3176].rearrange("p (k n) -> p k n", k=2),
                             A["ctxV"].rearrange("(k p) n -> p k n", p=P)),
                            (bvB, rows(A["L0_xattn_bv"], 1024))])
        t_wv = load(sp, [(wv, A["L0_xattn_Wv"].rearrange("(k p) n -> p k n", p=P))])
        t_wout = load(sp, [(wout[:, :, :], A["L0_attn_w_out"].rearrange("(k p) n -> p k n", p=P))])
        t_wq = load(sp, [(wq[:, :, :], A["L0_xattn_Wq"].rearrange("(k p) n -> p k n", p=P))])
        t_wo = load(sp, [(wo[:, :, :], A["L0_xattn_Wo"].rearrange("(k p) n -> p k n", p=P)),
                         (boB[:, :], rows(A["L0_xattn_bo"], D))])
        t_sm = load(sp, [(gw[:, :, :], A["gateT"]), (gbB[:, :], rows(A["L0_ffn_gate_b"], NE)),
                         (b13[:, :, :], A["b13"]),
                         (iot[:, :], A["iota"]), (eoff[:, :], A["eoff"]),
                         (slot[:, :], A["slot"]), (tokid[:, :], A["tokid"]),
                         (sw1[:, :, :], A["L0_ffn_sw1"].rearrange("(k p) n -> p k n", p=P)),
                         (sw3[:, :, :], A["L0_ffn_sw3"].rearrange("(k p) n -> p k n", p=P)),
                         (sw2[:, 0:2, :], A["L0_ffn_sw2"][0:256].rearrange("(k p) n -> p k n", p=P)),
                         (sw2[0:96, 2, :], A["L0_ffn_sw2"][256:352])])
        xs_sem = sem()
        xs_total = [0]
        xp_sem = sem()
        sp.dma(xp_sem, 16, xs[NE * RG:XROWS, :], A["pad"][NE * P:15 * P, :])

        t_kz = pool.do(lambda e: e.memset(kbd, 0.0))
        t_vz = pool.do(lambda e: e.memset(vbd, 0.0))
        t_on = pool.do(lambda e: e.memset(ones[:, :], 1.0))
        t_c0 = pool.do(lambda e: e.memset(cnt[:, 4, :], 0.0))

        xn_free = [()]
        ring = [0]
        xnT_free = [(), (), ()]

        def norm(c, ready):
            for i in range(4):
                t = 4 * c + i
                a = dve.do(lambda e, t=t, i=i: e.bn_stats(st[:, i, :], x[:, t, :]), *ready)
                a = dve.do(lambda e, i=i: e.bn_aggr(mv[:, i, :], st[:, i, :]), a)
            s = act.do(lambda e: e.activation(sd[:, :], mv[:, :, 1], ACT.Sqrt, bias=cst[:, 0:1]), a, t_id)
            r = dve.do(lambda e: e.reciprocal(rs[:, :], sd[:, :]), s)
            for i in range(4):
                t = 4 * c + i
                a = dve.do(lambda e, t=t, i=i: e.tensor_scalar(xn[:, i, 0:D], x[:, t, :], mv[:, i, 0:1],
                                                                rs[:, i:i + 1], ALU.subtract, ALU.mult),
                           r, *xn_free[0])
            xn_free[0] = ()
            return a

        def turned(a):
            r = ring[0] % 3
            ring[0] += 1
            done = []
            for k in range(2):
                n, ps, fr = bank()
                for i in range(4):
                    w = pe.do(lambda e, ps=ps, i=i, k=k: e.transpose(
                        ps[:, i * P:(i + 1) * P], xn[:, i, k * P:(k + 1) * P], ident[:, :]),
                        a, t_id, *fr, sig=(i == 3))
                g = act.do(lambda e, ps=ps, k=k, r=r: e.copy(xnT[:, r, k, :], ps[:, :]), w, *xnT_free[r])
                freed[n] = (g,)
                done.append(g)
            xn_free[0] += (w,)
            return r, tuple(done)

        decayed = []

        def decays():
            t_d = act.do(lambda e: e.activation(dec2[:, :, :], dec[:, :, :], ACT.Exp, scale=-1.0), t_cst)
            t_d = dve.do(lambda e: e.tensor_scalar(dec2[:, :, :], dec2[:, :, :], 1.0, None, ALU.add), t_d)
            t_d = dve.do(lambda e: e.reciprocal(dec2[:, :, :], dec2[:, :, :]), t_d)
            decayed.append(dve.do(lambda e: e.tensor_scalar(dec2[:, :, :], dec2[:, :, :], 1e-8, None, ALU.max), t_d))

        tmp_free = [()]
        den_free = [()]
        run_free = [(), ()]
        chunk_free = [()]
        carried = [None]
        lin = {}

        def scan(c, rT):
            r, xT = rT
            run = runs[c % 2]

            def project(blk):
                n, ps, fr = bank()
                for k in range(2):
                    w = pe.do(lambda e, ps=ps, k=k, blk=blk: e.matmul(
                        ps[:, :], wqkv[:, k, blk * P:(blk + 1) * P], xnT[:, r, k, :],
                        start=(k == 0), stop=(k == 1)), *xT, t_wqkv, *fr, sig=(k == 1))
                return n, ps, w

            tk = {}
            for name, first, buf in (("k", 2, kb), ("q", 0, qb)):
                for blk in range(2):
                    n, ps, w = project(first + blk)
                    act.do(lambda e, ps=ps: e.activation(tmp[:, 0:512], ps[:, :], ACT.Exp), w, *tmp_free[0])
                    e2 = act.do(lambda e, ps=ps: e.activation(tmp[:, 512:1024], ps[:, :], ACT.Relu))
                    freed[n] = (e2,)
                    g = dve.do(lambda e, buf=buf, blk=blk: e.scalar_tensor_tensor(
                        out=buf[:, blk, :], in0=tmp[:, 0:512], scalar=1.0, in1=tmp[:, 512:1024],
                        op0=ALU.min, op1=ALU.add), e2, *chunk_free[0])
                    tmp_free[0] = (g,)
                    tk[name, blk] = g
                    if name == "k":
                        n, ps, w = project(4 + blk)
                        g = dve.do(lambda e, ps=ps, blk=blk: e.tensor_tensor(
                            kvb[:, blk, :], ps[:, :], kb[:, blk, :], ALU.mult), w, g, *chunk_free[0])
                        freed[n] = (g,)
                        tk["kv", blk] = g
            xnT_free[r] = (w,)
            rt = {}
            for blk in range(2):
                for f in range(2):
                    j = 2 * f + blk
                    for w, src in ((0, kb), (1, kvb)):
                        init = 0.0 if c % 2 == 0 else carry[:, w, j:j + 1]
                        more = () if c % 2 == 0 else (carried[0],)
                        rt[w, j] = dve.do(lambda e, w=w, j=j, f=f, blk=blk, src=src, init=init: e.tensor_tensor_scan(
                            run[:, w, j, :], dec2[:, f, blk:blk + 1].broadcast_to([P, CT]), src[:, blk, :], init,
                            ALU.mult, ALU.add), decayed[0], tk["k", blk], tk["kv", blk], *run_free[c % 2], *more)
            more = ()
            if c % 2 == 0:
                carried[0] = dve.do(lambda e: e.tensor_copy(carry[:, :, 0:4], run[:, :, :, CT - 1]), rt[1, 3])
                more = (carried[0],)
            qk = {}
            for w in range(2):
                for j in range(4):
                    eng = pool if w == 1 else dve
                    qk[w, j] = eng.do(lambda e, w=w, j=j: e.tensor_tensor(
                        run[:, w, j, :], run[:, w, j, :], qb[:, j % 2, :], ALU.mult),
                        rt[w, j], tk["q", j % 2], *more)
            chunk_free[0] = (qk[1, 2], qk[1, 3])
            lin[c] = qk

        dens = {}
        shared = {}

        def summed(c):
            run = runs[c % 2]
            qk = lin[c]
            n, ps, fr = bank()
            for j in range(4):
                w = pe.do(lambda e, ps=ps, j=j: e.matmul(ps[:, :], sel[:, j, :], run[:, 0, j, :],
                                                         start=(j == 0), stop=(j == 3)),
                          qk[0, j], t_cst, *fr, sig=(j == 3))
            d = dve.do(lambda e, ps=ps: e.tensor_scalar(den, ps[:, :], 1e-6, None, ALU.max), w, *den_free[0])
            freed[n] = (d,)
            dens[c] = dve.do(lambda e: e.reciprocal(den, den), d)

        def divided(c):
            run = runs[c % 2]
            qk, d = lin[c], dens[c]
            on = shared[c] = []
            for j in range(4):
                n, ps, fr = bank()
                w = pe.do(lambda e, ps=ps, j=j: e.matmul(ps[:, :], selT[:, j, :], den, start=True, stop=True),
                          d, t_cst, *fr)
                g = dve.do(lambda e, ps=ps, j=j: e.tensor_tensor(
                    run[:, 1, j, :], ps[:, :], run[:, 1, j, :], ALU.mult), w, qk[1, j])
                freed[n] = (g,)
                on.append(g)
            den_free[0] = (w,)

        def mixed(c):
            run = runs[c % 2]
            on = shared[c]
            for t in range(4):
                n, ps, fr = bank()
                for j in range(4):
                    w = pe.do(lambda e, ps=ps, j=j, t=t: e.matmul(
                        ps[:, 0:D], run[:, 1, j, t * P:(t + 1) * P], wout[:, j, :],
                        start=(j == 0), stop=(j == 3)), on[j], t_wout, *fr, sig=(j == 3))
                g = dve.do(lambda e, ps=ps, c=c, t=t: e.tensor_tensor(
                    x[:, 4 * c + t, :], ps[:, 0:D], x[:, 4 * c + t, :], ALU.add), w)
                freed[n] = (g,)
            t_x[c] = g
            run_free[c % 2] = (w,)

        kv_done = []

        def keys():
            t_b = dve.do(lambda e: e.tensor_scalar(bq8[:, :], bqk[:, 0, :], 0.125, None, ALU.mult), t_ctx)
            for j in range(8):
                n, ps, fr = bank()
                for k in range(2):
                    w = pe.do(lambda e, ps=ps, k=k, j=j: e.matmul(
                        ps[:, 0:2 * SK], wk[:, k, j * P:(j + 1) * P], ctxT[:, k, :], start=(k == 0), stop=(k == 1)),
                        t_ctx, t_wk, *fr, sig=(k == 1))
                for b in range(B):
                    for r in range(2):
                        half = slice(64 * r, 64 * r + 64)
                        to = kbd[half, b, j, r * SK:(r + 1) * SK]
                        fro = ps[half, b * SK:(b + 1) * SK]
                        by = bqk[half, 1, j:j + 1]
                        if r:
                            t_k2 = dve.do(lambda e, to=to, fro=fro, by=by: e.tensor_scalar(
                                to, fro, by, None, ALU.add), w, t_kz)
                        else:
                            t_k = act.do(lambda e, to=to, fro=fro, by=by: e.activation(
                                to, fro, ACT.Identity, bias=by), w, t_kz)
                freed[n] = (t_k, t_k2)
            kv_done.extend([t_b, t_k, t_k2])

        groups = [(b, *g) for b in range(B) for g in (
            (0, 0, ((0, 128, 0, 0, 0),)),
            (1, 0, ((0, 32, 0, 1, 0), (32, 64, 1, 1, 1), (64, 128, 1, 1, 1))),
            (2, 1, ((0, 58, 1, 2, 1), (64, 128, 2, 3, 0))),
            (3, 2, ((0, 90, 2, 4, 0), (96, 128, 3, 4, 1))),
            (4, 3, ((0, 122, 3, 5, 1),)))]

        def contents(count):
            for b, t, h0, spans in [groups.pop(0) for _ in range(count)]:
                n, ps, fr = bank()
                hs = 1 if t in (0, 4) else 2
                for k in range(2):
                    w = pe.do(lambda e, ps=ps, k=k, b=b, t=t, h0=h0, hs=hs: e.matmul(
                        ps[:, 0:256 * hs], ctxV[:, k, b, t, :],
                        wv[:, k, :].rearrange("p (g n) -> p g n", g=4)[:, :, 64 * h0:64 * h0 + 64 * hs],
                        start=(k == 0), stop=(k == 1)), t_ctxV, t_wv, *fr, sig=(k == 1))
                for lo, hi, h, i, r in spans:
                    t_v = dve.do(lambda e, ps=ps, b=b, lo=lo, hi=hi, h=h, i=i, r=r, h0=h0, hs=hs: e.tensor_tensor(
                        vbd[lo:hi, b, :, i, 64 * r:64 * r + 64],
                        ps[lo:hi, 0:256 * hs].rearrange("p (g n) -> p g n", g=4)[:, :, 64 * (h - h0):64 * (h - h0) + 64],
                        bvB[lo:hi, :].rearrange("p (g n) -> p g n", g=4)[:, :, 64 * h:64 * h + 64], ALU.add), w, t_vz)
                freed[n] = (t_v,)
            kv_done[3:] = [t_v, w]

        fs_sem = [sem() for _ in range(2)]
        mk_sem = [sem() for _ in range(2)]
        mk_free = [(), ()]
        fs_free = [(), ()]
        att_free = [()] * 4
        q_free = [()]
        normed = {}
        probs = {}
        sided = {}
        over = {}
        top = {}

        def queries(u, rT):
            r, xT = rT
            c, cols = u // 2, slice(u % 2 * 256, u % 2 * 256 + 256)
            for t in (2 * u, 2 * u + 1):
                a = pool.do(lambda e, t=t: e.tensor_tensor(x[:, t, :], x[:, t, :], boB[:, :], ALU.add), *xT, t_wo)
            normed[u] = (a,)
            for j in range(8):
                n, ps, fr = bank()
                for k in range(2):
                    w = pe.do(lambda e, ps=ps, k=k, j=j: e.matmul(
                        ps[:, 0:256], wq[:, k, j * P:(j + 1) * P], xnT[:, r, k, cols], start=(k == 0), stop=(k == 1)),
                        *xT, t_wq, *fr, sig=(k == 1))
                g = act.do(lambda e, ps=ps, j=j: e.activation(qT[:, j, :], ps[:, 0:256], ACT.Identity,
                                                              bias=bq8[:, j:j + 1], scale=0.125),
                           w, kv_done[0], *q_free[0])
                freed[n] = (g,)
            xnT_free[r] = (w,)
            return (g,)

        def fetch(t):
            s = t % 2
            sp.dma(fs_sem[s], 0, fs[:, s, :, :], A["fside"][t], *fs_free[s])

        def fetch_mask(t):
            s = t % 2
            sp.dma(mk_sem[s], 0, mk[:, s, :, :], A["mask"][t], *mk_free[s])

        def scores(u, tq):
            for t in (2 * u, 2 * u + 1):
                b, s, a4 = t // 8, t % 2, t % 4
                tf = (fs_sem[s], 16 * (t // 2 + 1))
                for j in range(8):
                    n, ps, fr = bank()
                    w = pe.do(lambda e, ps=ps, j=j, b=b, t=t: e.matmul(
                        ps[:, 0:PW], qT[:, j, (t % 2) * P:(t % 2 + 1) * P], kbd[:, b, j, :], start=True, stop=True),
                        *tq, kv_done[1], kv_done[2], *fr)
                    g = dve.do(lambda e, ps=ps, j=j, s=s, a4=a4: e.tensor_tensor(
                        att[:, a4, 2 * j:2 * j + 2, 0:SK],
                        ps[:, 0:PW].rearrange("p (r k) -> p r k", r=2),
                        fs[:, s, 2 * j:2 * j + 2, :], ALU.mult), w, tf, *att_free[a4])
                    freed[n] = (g,)
                q_free[0] = (w,)
                sided[t] = g

        def masked(t):
            s, a4 = t % 2, t % 4
            over[t] = dve.do(lambda e: e.scalar_tensor_tensor(
                out=att[:, a4, :, 0:SK], in0=mk[:, s, :, :], scalar=-BIG, in1=att[:, a4, :, 0:SK],
                op0=ALU.mult, op1=ALU.add), sided[t], (mk_sem[s], 16 * (t // 2 + 1)))
            fs_free[s] = (sided[t],)
            mk_free[s] = (over[t],)
            if t + 2 < NT:
                fetch(t + 2)
                fetch_mask(t + 2)

        def topped(t):
            a4 = t % 4
            g = dve.do(lambda e: e.tensor_reduce(mx[:, a4, 0, :], att[:, a4, :, 0:SK], AX.X, ALU.max), over[t])
            g = dve.do(lambda e: e.tensor_scalar(mx[:, a4, 1, :], mx[:, a4, 0, :], -1.0e38, -BIG,
                                                 ALU.is_le, ALU.mult), g)
            top[t] = dve.do(lambda e: e.scalar_tensor_tensor(
                out=mx[:, a4, 1, :], in0=mx[:, a4, 1, :], scalar=BIG, in1=mx[:, a4, 0, :],
                op0=ALU.mult, op1=ALU.subtract), g)

        def raised(t, heads):
            a4 = t % 4
            for h in heads:
                probs[t] = act.do(lambda e, h=h: e.activation(
                    att[:, a4, h, 0:SK], att[:, a4, h, 0:SK], ACT.Exp,
                    bias=mx[:, a4, 1, h:h + 1], accum_out=mx[:, a4, 2, h:h + 1]), top[t])

        def scaled(t):
            a4 = t % 4
            e1 = probs[t]
            g = dve.do(lambda e: e.reciprocal(mx[:, a4, 3, :], mx[:, a4, 2, :]), e1)
            probs[t] = pool.do(lambda e: e.tensor_tensor(
                att[:, a4, :, 0:SK], att[:, a4, :, 0:SK],
                mx[:, a4, 3, :].rearrange("p (h a) -> p h a", a=1).broadcast_to([P, H, SK]), ALU.mult), g, e1)

        def softmax(u, more):
            t0, t1 = 2 * u, 2 * u + 1
            masked(t0)
            topped(t0)
            return [lambda: None,
                    lambda: (masked(t1), topped(t1), raised(t0, range(0, 5))),
                    lambda: raised(t0, range(5, 11)),
                    lambda: raised(t0, range(11, 16)),
                    lambda: (more(), scaled(t0), raised(t1, range(0, 8))),
                    lambda: (raised(t1, range(8, 16)), scaled(t1))]

        pT_free = [(), ()]
        oT_free = [()]

        def values(u, between):
            b = u // 4
            oc = []
            pend = None

            def product(jj, s, ev):
                n, ps, fr = bank()
                for i in range(2):
                    for m in range(3):
                        w2 = pe.do(lambda e, ps=ps, i=i, m=m, jj=jj, s=s: e.matmul(
                            ps[:, i * 256:(i + 1) * 256], vbd[:, b, jj, 3 * i + m, :], pT[:, s, 2 * i + m, :],
                            start=(m == 0), stop=(m == 2)), *ev, kv_done[3], *fr, sig=(m == 2))
                pT_free[s] = (w2,)
                g = dve.do(lambda e, ps=ps, jj=jj: e.tensor_copy(
                    oT[:, 2 * jj:2 * jj + 2, :], ps[:, :].rearrange("p (i q) -> p i q", i=2)), w2, *oT_free[0])
                freed[n] = (g,)
                oc.append(g)

            for jj in range(4):
                s = jj % 2
                ev = []
                for t0, ts in ((0, 2), (2, 2), (4, 1)):
                    n, ps, fr = bank()
                    for tt in range(t0, t0 + ts):
                        for q in range(2):
                            a4 = (2 * u + q) % 4
                            w = pe.do(lambda e, ps=ps, a4=a4, jj=jj, tt=tt, t0=t0, q=q: e.transpose(
                                ps[:, (2 * (tt - t0) + q) * P:(2 * (tt - t0) + q + 1) * P],
                                att[:, a4, 4 * jj:4 * jj + 4, :].rearrange("p r k -> p (r k)")[
                                    :, tt * P:(tt + 1) * P], ident[:, :]),
                                probs[2 * u + q], *fr, sig=(q == 1))
                    g = act.do(lambda e, ps=ps, s=s, t0=t0, ts=ts: e.copy(
                        pT[:, s, t0:t0 + ts, :], ps[:, 0:256 * ts].rearrange("p (t q) -> p t q", t=ts)),
                        w, *pT_free[s])
                    freed[n] = (g,)
                    ev.append(g)
                if pend:
                    product(*pend)
                pend = (jj, s, ev)
                if between:
                    between.pop(0)()
            for q in range(2):
                att_free[(2 * u + q) % 4] = (w,)
            product(*pend)
            if between:
                between.pop(0)()
            for q in range(2):
                t = 2 * u + q
                n, ps, fr = bank()
                for j in range(8):
                    w = pe.do(lambda e, ps=ps, j=j, q=q: e.matmul(
                        ps[:, 0:D], oT[:, j, q * P:(q + 1) * P], wo[:, j, :], start=(j == 0), stop=(j == 7)),
                        oc[j // 2], t_wo, *fr, sig=(j == 7))
                g = dve.do(lambda e, ps=ps, t=t: e.tensor_tensor(x[:, t, :], ps[:, 0:D], x[:, t, :], ALU.add),
                           w, *normed[u])
                freed[n] = (g,)
            oT_free[0] = (w,)
            t_x[u // 2] = g
            for part in between:
                part()

        def per_token(v):
            return v.rearrange("p (t a) -> p t a", a=1).broadcast_to([P, 4, NE])

        def per_expert(v):
            return v.rearrange("p (a n) -> p a n", a=1).broadcast_to([P, 4, NE])

        def dstep(fn, *waits):
            return dve.do(fn, (dve.sem, dve.count), *waits)

        x3 = {}
        n3 = {}
        added = {}
        gate_done = {}

        def third(c):
            a = n3[c]
            x3[c] = turned(a)
            for t in range(4 * c, 4 * c + 4):
                a2 = pool.do(lambda e, t=t: e.tensor_tensor(x[:, t, :], x[:, t, :], sb2B, ALU.add), a, t_s2)
            added[c] = (a2,)

        def gate(c):
            r, xT = x3[c]
            n, ps, fr = bank()
            for i in range(4):
                for k in range(2):
                    w = pe.do(lambda e, ps=ps, k=k, i=i: e.matmul(
                        ps[:, NE * i:NE * i + NE], xnT[:, r, k, i * P:(i + 1) * P], gw[:, k, :],
                        start=(k == 0), stop=(k == 1)), *xT, t_sm, *fr, sig=(k == 1))
            p1, p2 = o1[:, 4 * c:4 * c + 4, :], o2[:, 4 * c:4 * c + 4, :]
            lg4 = ps[:, 0:4 * NE].rearrange("p (t n) -> p t n", t=4)
            ids = dve.do(lambda e: e.tensor_copy(xn[:, :, D].bitcast(I32), tokid[:, 4 * c:4 * c + 4]),
                         t_sm, *xn_scattered[0])
            dstep(lambda e: e.tensor_reduce(gm[:, :], lg4, AX.X, ALU.max), w)
            g = dstep(lambda e: e.tensor_tensor(lg[:, :, :], lg4, per_token(gm[:, :]), ALU.subtract))
            freed[n] = (g,)
            w = act.do(lambda e: e.activation(lg[:, :, :], lg[:, :, :], ACT.Exp), g)
            dstep(lambda e: e.tensor_reduce(gm[:, :], lg[:, :, :], AX.X, ALU.add), w)
            dstep(lambda e: e.reciprocal(gm[:, :], gm[:, :]))
            dstep(lambda e: e.tensor_tensor(lg[:, :, :], lg[:, :, :], per_token(gm[:, :]), ALU.mult))
            dstep(lambda e: e.tensor_tensor(ga[:, :, :], lg[:, :, :], per_expert(gbB[:, :]), ALU.add))
            for i, o in enumerate((p1, p2)):
                dstep(lambda e: e.tensor_reduce(gm[:, :], ga[:, :, :], AX.X, ALU.max))
                dstep(lambda e: e.tensor_tensor(gt[:, :, :], ga[:, :, :], per_token(gm[:, :]), ALU.is_ge))
                dstep(lambda e: e.tensor_tensor(gt[:, :, :], gt[:, :, :], per_expert(iot[:, :]), ALU.mult))
                dstep(lambda e: e.tensor_reduce(gm[:, :], gt[:, :, :], AX.X, ALU.max))
                dstep(lambda e, o=o: e.tensor_tensor(o, per_expert(iot[:, :]), per_token(gm[:, :]), ALU.is_equal))
                dstep(lambda e, o=o: e.tensor_tensor(gt[:, :, :], o, lg[:, :, :], ALU.mult))
                dstep(lambda e, i=i: e.tensor_reduce(wsel[:, i, :], gt[:, :, :], AX.X, ALU.add))
                if i == 0:
                    dstep(lambda e, o=o: e.scalar_tensor_tensor(
                        out=ga[:, :, :], in0=o, scalar=-BIG, in1=ga[:, :, :], op0=ALU.mult, op1=ALU.add))
            ids = dstep(lambda e: e.tensor_copy(xn[:, :, D + 1], wsel[:, 0, :]), ids)
            g = dstep(lambda e: e.tensor_tensor(gt[:, :, :], p1, p2, ALU.add))
            gate_done[c] = (g, ids)

        xn_scattered = [()]

        def placed(c):
            g, ids = gate_done[c]
            n, ps, fr = bank()
            gt2 = gt[:, :, :].rearrange("p t n -> p (t n)")
            pe.do(lambda e, ps=ps: e.matmul(ps[:, 0:32], tri, gt2, start=True, stop=True),
                  g, t_s2, *fr, sig=False)
            w = pe.do(lambda e, ps=ps: e.matmul(ps[:, 32:64], ones[:, :], gt2, start=True, stop=True), t_on)
            dstep(lambda e: e.tensor_copy(cnt[:, 0, :], cnt[:, 4, :]), t_c0)
            for i in range(4):
                dstep(lambda e, i=i, ps=ps: e.tensor_tensor(
                    cnt[:, i + 1, :], ps[:, 32 + NE * i:32 + NE * i + NE], cnt[:, i, :], ALU.add), w)
            p4 = ps[:, 0:32].rearrange("p (t n) -> p t n", t=4)
            g = dstep(lambda e, p4=p4: e.tensor_tensor(ga[:, :, :], p4, cnt[:, 0:4, :], ALU.add))
            freed[n] = (g,)
            dstep(lambda e: e.tensor_tensor(ga[:, :, :], ga[:, :, :], per_expert(eoff[:, :]), ALU.add))
            for i, o in enumerate((o1, o2)):
                dstep(lambda e, o=o: e.tensor_tensor(gt[:, :, :], ga[:, :, :], o[:, 4 * c:4 * c + 4, :], ALU.mult))
                dstep(lambda e, i=i: e.tensor_reduce(posf[:, i, :], gt[:, :, :], AX.X, ALU.add))
            g = dstep(lambda e: e.tensor_copy(pos[:, c, :, :], posf[:, :, :]))
            for k in range(2):
                if k == 1:
                    ids = pool.do(lambda e: e.tensor_copy(xn[:, :, D + 1], wsel[:, 1, :]),
                                 (xs_sem, xs_total[0]))
                xs_total[0] += 64
                for i in range(4):
                    pool.items.append(((g, ids), lambda e, i=i, k=k: e.indirect_dma_start(
                        out=xs, out_offset=bass.IndirectOffsetOnAxis(
                            ap=pos[:, c, k, i:i + 1].bitcast(U32), axis=0),
                        in_=xn[:, i, :], in_offset=None).then_inc(xs_sem, 16), False))
            xn_scattered[0] = ((xs_sem, xs_total[0]),)
            xn_free[0] += xn_scattered[0]

        hA_free = [(), ()]
        hZ_free = [(), ()]
        part = {}

        def shared_in(c, half):
            shared_mm(c, half)
            shared_act(c, half)

        def shared_mm(c, half):
            r, xT = x3[c]
            cols = slice(half * 256, half * 256 + 256)
            got = part[c, half] = []
            for m, (lo, mw) in enumerate(MT):
                n, ps, fr = bank()
                for q, wm in enumerate((sw1, sw3)):
                    for k in range(2):
                        w = pe.do(lambda e, ps=ps, k=k, wm=wm, lo=lo, mw=mw, q=q: e.matmul(
                            ps[0:mw, q * 256:q * 256 + 256], wm[:, k, lo:lo + mw], xnT[:, r, k, cols],
                            start=(k == 0), stop=(k == 1)), *xT, t_sm, *fr, sig=(q == 1 and k == 1))
                got.append((n, ps, w))
            xnT_free[r] = (w,)

        def shared_act(c, half):
            zt = []
            for m, (lo, mw) in enumerate(MT):
                n, ps, w = part[c, half][m]
                a = act.do(lambda e, ps=ps, m=m, mw=mw: e.activation(
                    hA[0:mw, :], ps[0:mw, 0:256], ACT.Identity, bias=b13[0:mw, 0, m:m + 1]), w, *hA_free[0])
                g = dve.do(lambda e, ps=ps, m=m, mw=mw: e.scalar_tensor_tensor(
                    out=hZ[0:mw, m, :], in0=ps[0:mw, 256:512], scalar=b13[0:mw, 1, m:m + 1],
                    in1=hA[0:mw, :], op0=ALU.add, op1=ALU.mult), a, *hZ_free[0])
                freed[n] = (g,)
                hA_free[0] = (g,)
                zt.append(act.do(lambda e, m=m, mw=mw: e.activation(
                    hZ[0:mw, m, :], hZ[0:mw, m, :], ACT.Silu), g))
            part[c, half] = zt

        def shared_out(c, half):
            zt = part[c, half]
            for i in range(2):
                t = 4 * c + 2 * half + i
                n, ps, fr = bank()
                for m, (lo, mw) in enumerate(MT):
                    w = pe.do(lambda e, ps=ps, m=m, mw=mw, i=i: e.matmul(
                        ps[:, 0:D], hZ[0:mw, m, i * P:(i + 1) * P], sw2[0:mw, m, :],
                        start=(m == 0), stop=(m == 2)), zt[m], *fr, sig=(m == 2))
                g = dve.do(lambda e, ps=ps, t=t: e.tensor_tensor(x[:, t, :], ps[:, 0:D], x[:, t, :], ALU.add),
                           w, *added[c])
                freed[n] = (g,)
                t_x[c] = g
            hZ_free[0] = (w,)

        a = norm(0, (t_x[0],))
        r0 = turned(a)
        keys()
        decays()
        a = norm(1, (t_x[1],))
        scan(0, r0)
        r1 = turned(a)
        contents(3)
        summed(0)
        a = norm(2, (t_x[2],))
        contents(3)
        divided(0)
        scan(1, r1)
        r2 = turned(a)
        mixed(0)
        summed(1)
        contents(2)
        a = norm(3, (t_x[3],))
        divided(1)
        scan(2, r2)
        r3 = turned(a)
        mixed(1)
        summed(2)
        contents(2)
        a = norm(0, (t_x[0],))
        divided(2)
        scan(3, r3)
        rT = turned(a)
        mixed(2)
        a = norm(1, (t_x[1],))
        summed(3)
        early = run_free[0] + chunk_free[0] + tmp_free[0] + tuple(kv_done)
        q_free[0] = early
        tq = queries(0, rT)
        divided(3)
        t_az = pool.do(lambda e: e.memset(att[:, 0:2, :, SK:HK], 0.0), *early)
        att_free[0:2] = [early + (t_az,)] * 2
        fs_free[:] = [early, early]
        mk_free[:] = [early, early + den_free[0]]
        for t in range(2):
            fetch(t)
            fetch_mask(t)
        scores(0, tq)
        for t in range(2):
            masked(t)
            topped(t)
        tq = queries(1, rT)
        raised(0, range(H))
        mixed(3)
        rN = turned(a)
        raised(1, range(H))
        late = early + run_free[1] + den_free[0]
        t_az = pool.do(lambda e: e.memset(att[:, 2:4, :, SK:HK], 0.0), *late)
        att_free[2:4] = [late + (t_az,)] * 2
        pT_free[:] = [late, late]
        oT_free[0] = late
        t_s2 = load(sp, [(sb2B, rows(A["L0_ffn_sb2"], D)), (tri, A["tri"])], *late)
        fill = {3: (0, 0), 4: (0, 1), 5: (1, 0), 6: (1, 1), 7: (2, 0)}
        scaled(0)
        for u in range(1, 8):
            scores(u, tq)
            if u == 1:
                scaled(1)
            if u % 2 == 0 and u < 6:
                rN = turned(a)
            gating = u >= 3 and u % 2 == 1
            values(u - 1, softmax(u, lambda: gate((u - 3) // 2) if gating else None))
            if u >= 3 and u % 2 == 1:
                placed((u - 3) // 2)
            if u % 2 == 0:
                n3[u // 2 - 1] = norm(u // 2 - 1, (t_x[u // 2 - 1],))
            if u in fill:
                shared_in(*fill[u])
            if u % 2 == 1:
                rT = rN
            if u < 7:
                tq = queries(u + 1, rT)
            if u in fill:
                shared_out(*fill[u])
            if u % 2 == 0:
                third(u // 2 - 1)
            if u in (1, 3):
                a = norm(u // 2 + 2, (t_x[u // 2 + 2],))
        t_r3 = mk_free[0] + mk_free[1]
        ew_sem, ew2_sem = sem(), sem()

        def fetch_w13(experts, *waits):
            for ex in experts:
                for q, wm in enumerate(("L0_ffn_w1", "L0_ffn_w3")):
                    sp.dma(ew_sem, 0, ew13[:, ex * 1408 + q * 704:ex * 1408 + q * 704 + 704].rearrange(
                        "p (k n) -> p k n", k=2), A[wm][ex].rearrange("(k p) n -> p k n", p=P), *waits)

        fetch_w13(range(5), *q_free[0], *att_free[0], *att_free[1])
        for ex in range(NE):
            d = ew2_sem
            sp.dma(d, 0, ew2[:, ex * 768:ex * 768 + 512].rearrange("p (k n) -> p k n", k=2),
                   A["L0_ffn_w2"][ex, 0:256].rearrange("(k p) n -> p k n", p=P), *t_r3)
            sp.dma(d, 0, ew2[0:96, ex * 768 + 512:ex * 768 + 768], A["L0_ffn_w2"][ex, 256:352])
        values(7, [])
        late = att_free[2] + att_free[3] + oT_free[0] + pT_free[0] + pT_free[1]
        fetch_w13(range(5, NE), *late)
        sp.dma(ew_sem, 0, eb, A["ebias"].broadcast_to([P, NE * 960]), *late)
        t_ew2 = (ew2_sem, 256)
        t_ew = (ew_sem, 272)
        n3[3] = norm(3, (t_x[3],))
        shared_mm(2, 1)
        third(3)
        gate(3)
        placed(3)
        shared_act(2, 1)
        shared_mm(3, 0)

        late = att_free[3] + oT_free[0] + pT_free[0] + pT_free[1]

        n_e = cnt[:, 4, :]
        dstep(lambda e: e.tensor_tensor(ntf[:, :], n_e, eoff[:, :], ALU.add))
        t_pr = dstep(lambda e: e.tensor_copy(prow[:, :], ntf[:, :]))
        dstep(lambda e: e.tensor_scalar(ntf[:, :], n_e, 127.0, None, ALU.add))
        dstep(lambda e: e.tensor_copy(nti[:, :], ntf[:, :]))
        dstep(lambda e: e.tensor_single_scalar(nti[:, :], nti[:, :], 7, ALU.logical_shift_right))
        dstep(lambda e: e.tensor_copy(ntf[:, :], nti[:, :]))
        dstep(lambda e: e.tensor_tensor_scan(end[:, :], ones[:, 0:NE], ntf[:, :], 0.0, ALU.mult, ALU.add))

        def by_slot(v):
            return v.rearrange("p (s a) -> p s a", a=1).broadcast_to([P, NS, NE])

        def by_end(v):
            return v.rearrange("p (a n) -> p a n", a=1).broadcast_to([P, NS, NE])

        dstep(lambda e: e.tensor_tensor(cmp_[:, :, :], by_slot(slot[:, :]), by_end(end[:, :]), ALU.is_ge))
        dstep(lambda e: e.tensor_reduce(se[:, 0, :], cmp_[:, :, :], AX.X, ALU.add))
        dstep(lambda e: e.tensor_tensor(cmp_[:, :, :], cmp_[:, :, :], by_end(end[:, :]), ALU.mult))
        dstep(lambda e: e.tensor_reduce(se[:, 1, :], cmp_[:, :, :], AX.X, ALU.max))
        dstep(lambda e: e.tensor_tensor(se[:, 1, :], slot[:, :], se[:, 1, :], ALU.subtract))
        dstep(lambda e: e.tensor_scalar(se[:, 1, :], se[:, 1, :], float(P), None, ALU.mult))
        dstep(lambda e: e.scalar_tensor_tensor(out=se[:, 1, :], in0=se[:, 0, :], scalar=float(RG), in1=se[:, 1, :],
                                               op0=ALU.mult, op1=ALU.add))
        dstep(lambda e: e.tensor_scalar(se[:, 0, :], se[:, 0, :], float(NE - 1), None, ALU.min))
        t_sl = dstep(lambda e: e.tensor_copy(sei[:, :, :], se[:, 0:2, :]))

        shared_out(2, 1)
        shared_act(3, 0)
        shared_mm(3, 1)
        shared_out(3, 0)
        shared_act(3, 1)
        shared_out(3, 1)

        def pad(ex):
            def go(e):
                v = e.value_load(prow[0:1, ex:ex + 1], min_val=ex * RG, max_val=ex * RG + N)
                return e.dma_start(xs[bass.ds(v, P), :], A["pad"][ex * P:(ex + 1) * P, :]).then_inc(xp_sem, 16)
            return go

        for ex in range(NE):
            sp.items.append(((t_pr,), pad(ex), False))
        t_xs = (xs_sem, xs_total[0])
        t_xp = (xp_sem, 16 + 16 * NE)

        xl_sem = [sem() for _ in range(6)]
        zr_sem = sem()
        xsl_free = [late] * 6
        xsT_free = [late] * 2
        sA_free = [late] * 2
        sT_free = [late] * 2
        sY_free = [late] * 4
        w_reg, b_reg = {}, {}
        flip, hid, hidT = {}, {}, {}

        def read(s):
            def go(e):
                v = e.value_load(sei[0:1, 1, s:s + 1], min_val=0, max_val=XROWS - P)
                return e.dma_start(xsl[:, s % 6, :], xs[bass.ds(v, P), :]).then_inc(xl_sem[s % 6], 16)
            sp.items.append(((t_sl, t_xs, t_xp, *xsl_free[s % 6]), go, False))

        def rows_turned(s):
            i2 = s % 2
            n, ps, fr = bank()
            for k in range(2):
                w = pe.do(lambda e, ps=ps, k=k: e.transpose(ps[:, k * P:(k + 1) * P],
                                                            xsl[:, s % 6, k * P:(k + 1) * P], ident[:, :]),
                          (xl_sem[s % 6], 16 * (s // 6 + 1)), *fr, sig=(k == 1))
            g = act.do(lambda e, ps=ps: e.copy(xsT[:, i2, :, :], ps[:, 0:256].rearrange("p (k q) -> p k q", k=2)),
                       w, *xsT_free[i2])
            freed[n] = (g,)
            flip[s] = g

        def hidden(s):
            i2 = s % 2

            def pick(e):
                w_reg[s] = e.value_load(sei[0:1, 0, s:s + 1], min_val=0, max_val=NE - 1)

            def pickb(e):
                b_reg[s] = e.value_load(sei[0:1, 0, s:s + 1], min_val=0, max_val=NE - 1)

            pe.items.append(((t_sl,), pick, False))
            dve.items.append(((t_sl,), pickb, False))
            ws = []
            for q in range(2):
                n, ps, fr = bank()
                for k in range(2):
                    w = pe.do(lambda e, ps=ps, k=k, q=q: e.matmul(
                        ps[:, 0:F], xsT[:, i2, k, :], ew13[:, bass.ds(w_reg[s] * 1408 + q * 704 + k * F, F)],
                        start=(k == 0), stop=(k == 1)), flip[s], t_ew, *fr, sig=(k == 1))
                ws.append((n, ps, w))
            xsT_free[i2] = (w,)
            n, ps, w = ws[0]
            a = dve.do(lambda e, ps=ps: e.tensor_tensor(sA[:, i2, :], ps[:, 0:F], eb[:, bass.ds(b_reg[s] * 960, F)],
                                                        ALU.add), w, t_ew, *sA_free[i2])
            freed[n] = (a,)
            n, ps, w = ws[1]
            z = dve.do(lambda e, ps=ps: e.tensor_tensor(sZ[:, i2, :], ps[:, 0:F],
                                                        eb[:, bass.ds(b_reg[s] * 960 + F, F)], ALU.add), w)
            freed[n] = (z,)
            z = dve.do(lambda e: e.tensor_tensor(sZ[:, i2, :], sZ[:, i2, :], sA[:, i2, :], ALU.mult), a, z)
            hid[s] = act.do(lambda e: e.activation(sZ[:, i2, :], sZ[:, i2, :], ACT.Silu), z)

        def hidden_turned(s):
            i2 = s % 2
            n, ps, fr = bank()
            for m, (lo, mw) in enumerate(MT):
                w = pe.do(lambda e, ps=ps, m=m, lo=lo, mw=mw: e.transpose(
                    ps[0:mw, m * P:(m + 1) * P], sZ[:, i2, lo:lo + mw], ident[:, :]), hid[s], *fr, sig=(m == 2))
            sA_free[i2] = (w,)
            act.do(lambda e, ps=ps: e.copy(sT[:, i2, 0:2, :], ps[:, 0:256].rearrange("p (m q) -> p m q", m=2)),
                   w, *sT_free[i2])
            g = act.do(lambda e, ps=ps: e.copy(sT[0:96, i2, 2, :], ps[0:96, 256:384]))
            freed[n] = (g,)
            hidT[s] = g

        def results(s):
            i2 = s % 2
            n, ps, fr = bank()
            for m, (lo, mw) in enumerate(MT):
                w = pe.do(lambda e, ps=ps, m=m, mw=mw: e.matmul(
                    ps[:, 0:D], sT[0:mw, i2, m, :], ew2[0:mw, bass.ds(w_reg[s] * 768 + m * D, D)],
                    start=(m == 0), stop=(m == 2)), hidT[s], t_ew2, *fr, sig=(m == 2))
            sT_free[i2] = (w,)
            g = dve.do(lambda e, ps=ps: e.tensor_tensor(sY[:, s % 4, :], ps[:, 0:D],
                                                        eb[:, bass.ds(b_reg[s] * 960 + 2 * F, D)], ALU.add),
                       w, *sY_free[s % 4])
            freed[n] = (g,)
            g = dve.do(lambda e: e.tensor_scalar(sY[:, s % 4, :], sY[:, s % 4, :], xsl[:, s % 6, D + 1:D + 2], None,
                                                 ALU.mult), g)
            before = (zr_sem, 16 * s) if s else t_base
            pool.items.append(((g, before), lambda e: e.indirect_dma_start(
                out=zs, out_offset=bass.IndirectOffsetOnAxis(ap=xsl[:, s % 6, D:D + 1].bitcast(U32), axis=0),
                in_=sY[:, s % 4, :], in_offset=None, compute_op=ALU.add).then_inc(zr_sem, 16), False))
            done = (zr_sem, 16 * s + 16)
            sY_free[s % 4] = (done,)
            xsl_free[s % 6] = (done,)

        for s in range(4):
            read(s)
        zi_sem = sem()
        sp.dma(zi_sem, 16, zs[N:ZROWS, :], A["x"].rearrange("b s d -> (b s) d")[0:ZROWS - N, :])
        for c in range(NCH):
            sp.dma(zi_sem, 16, zs[c * CT:c * CT + CT, :].rearrange("(t p) d -> p t d", p=P), x[:, 4 * c:4 * c + 4, :],
                   t_x[c])
        t_base = (zi_sem, 16 + 16 * NCH)
        rows_turned(0)
        for s in range(NS + 2):
            if s + 1 < NS:
                rows_turned(s + 1)
            if s < NS:
                hidden(s)
            if 1 <= s <= NS:
                hidden_turned(s - 1)
            if s >= 2:
                results(s - 2)
            if s + 4 < NS:
                read(s + 4)
        o_sem = sem()
        half = N // 2
        outr = out.rearrange("b s d -> (b s) d")
        for i, q in enumerate((sp, act)):
            q.dma(o_sem, 32, outr[i * half:(i + 1) * half, :], zs[i * half:(i + 1) * half, :], (zr_sem, 16 * NS))
        act.wait((o_sem, 32))

        block = ctx.enter_context(nc.Block())

        @block.sync
        def _(eng):
            sp.play(eng)

        @block.scalar
        def _(eng):
            act.play(eng)

        @block.gpsimd
        def _(eng):
            pool.play(eng)

        @block.vector
        def _(eng):
            dve.play(eng)

        @block.tensor
        def _(eng):
            pe.play(eng)


def layout(inputs):
    a = {k: np.ascontiguousarray(v) for k, v in inputs.items()}
    o = {k: a[k] for k in ("x", "L0_attn_w_qkv", "L0_attn_w_out", "L0_xattn_Wq", "L0_xattn_Wk", "L0_xattn_Wv",
                           "L0_xattn_Wo", "L0_xattn_bv", "L0_xattn_bo", "L0_ffn_gate_b", "L0_ffn_w1", "L0_ffn_w3",
                           "L0_ffn_w2", "L0_ffn_sw1", "L0_ffn_sw3", "L0_ffn_sw2", "L0_ffn_sb2")}
    ctx = a["ctx_1024"]
    o["ctxT"] = np.ascontiguousarray(ctx.reshape(B * SK, D).T)
    cv = np.zeros((D, B, 5, P), ctx.dtype)
    for b in range(B):
        t = ctx[b].T
        for h in range(4):
            at = HK * h
            for i in range(5):
                lo, hi = max(at, P * i), min(at + SK, P * i + P)
                if lo < hi:
                    cv[:, b, i, lo - P * i:hi - P * i] = t[:, lo - at:hi - at]
    o["ctxV"] = cv.reshape(D, B * 5 * P)
    o["fside"] = np.ascontiguousarray(
        a["fside_Bx16xSxS2_0"].reshape(B, H, 8, P, SK).transpose(0, 2, 3, 1, 4)).reshape(NT, P, H, SK)
    o["mask"] = np.ascontiguousarray(
        a["mask_Bx16xSxS2_bk1"].reshape(B, H, 8, P, SK).transpose(0, 2, 3, 1, 4)).reshape(NT, P, H, SK)
    ab = np.stack([a["L0_attn_alpha"], a["L0_attn_beta"]])
    o["decay"] = np.ascontiguousarray(np.repeat(ab, 16, axis=1).reshape(2, 2, P).transpose(2, 0, 1))
    bqk = np.stack([a["L0_xattn_bq"], a["L0_xattn_bk"]])
    o["bqk"] = np.ascontiguousarray(bqk.reshape(2, 8, P).transpose(2, 0, 1))
    o["gateT"] = np.ascontiguousarray(a["L0_ffn_gate_w"].T.reshape(2, P, NE).transpose(1, 0, 2))
    b13 = np.zeros((2, 384), np.float32)
    b13[0, 0:F], b13[1, 0:F] = a["L0_ffn_sb1"], a["L0_ffn_sb3"]
    o["b13"] = np.ascontiguousarray(b13.reshape(2, 3, P).transpose(2, 0, 1))
    sel = np.zeros((P, 4, P), np.float32)
    for j in range(4):
        for p in range(P):
            sel[p, j, 8 * j + p // 16::32] = 1.0
    o["sel"] = sel
    o["selT"] = np.ascontiguousarray(sel.transpose(2, 1, 0)) * np.float32(0.25)
    o["ident"] = np.eye(P, dtype=np.float32)
    o["cst"] = np.full((P, 2), 1e-5, np.float32)
    o["tri"] = np.triu(np.ones((P, P), np.float32), 1)
    o["eoff"] = np.tile(np.arange(NE).astype(np.float32) * RG, (P, 1))
    o["slot"] = np.tile(np.arange(NS).astype(np.float32), (P, 1))
    tok = np.arange(N, dtype=np.int32).reshape(NT, P).T
    o["tokid"] = np.ascontiguousarray(tok)
    pad = np.zeros((15 * P, XW), np.float32)
    pad.view(np.int32)[:, D] = N + np.arange(15 * P, dtype=np.int32)
    o["pad"] = pad
    bias = np.zeros((NE, 960), np.float32)
    bias[:, 0:F], bias[:, F:2 * F], bias[:, 2 * F:] = a["L0_ffn_b1"], a["L0_ffn_b3"], a["L0_ffn_b2"]
    o["ebias"] = bias.reshape(1, NE * 960)
    o["iota"] = np.tile(np.arange(8, 0, -1).astype(np.float32), (P, 1))
    return o


def kernel(**inputs):
    import concourse.bacc as _bacc
    from concourse.bass_utils import run_bass_kernel_spmd as _run

    nc = _bacc.Bacc("TRN2", target_bir_lowering=False, num_devices=1)
    arrays, aps = {}, {}
    for name, a in layout(inputs).items():
        arrays[f"in_{name}_dram"] = a
        aps[name] = nc.dram_tensor(f"in_{name}_dram", a.shape, mybir.dt.from_np(a.dtype), kind="ExternalInput").ap()
    out = nc.dram_tensor("out_0_dram", (B, S, D), F32, kind="ExternalOutput").ap()
    xs = nc.dram_tensor("xs_dram", (XROWS, XW), F32, kind="Internal").ap()
    zs = nc.dram_tensor("zs_dram", (ZROWS, D), F32, kind="Internal").ap()
    decoder(nc, aps, xs, zs, out)
    r = _run(nc, [arrays], core_ids=[0])
    return r.results[0]["out_0_dram"]
```
